# Optimizing a Trainium2 kernel written in Bass

```python
import numpy as np
import jax
import jax.numpy as jnp

def _softmax(x, axis=-1):
    return jax.nn.softmax(x, axis=axis)

def _gelu(x):
    return jax.nn.gelu(x, approximate=True)

def _silu(x):
    return jax.nn.silu(x)

def _sigmoid(x):
    return jax.nn.sigmoid(x)

def _layernorm(x, axis=-1, eps=1e-05):
    m = jnp.mean(x, axis=axis, keepdims=True)
    v = jnp.var(x, axis=axis, keepdims=True)
    return (x - m) / jnp.sqrt(v + eps)

def _scatter_add(tgt, idx, src, axis=0):
    return tgt.at[idx].add(src)

def _segment_sum(src, seg, n):
    return jax.ops.segment_sum(src, seg, n)
kernel_name = 'mk_gnn_preln_d4_gnn_r16_f1779c'

def setup_inputs(seed: int=0):
    np.random.seed(seed)
    _w = jnp.asarray

    def _rec_inputs():
        import jax
        import jax.numpy as jnp
        _gk = jax.random.key(seed)
        x = -8.776e-05 + 1 * jax.random.normal(jax.random.fold_in(_gk, 1), (625, 512), jnp.float32)
        _s = jax.random.randint(jax.random.fold_in(_gk, 2), (10000,), 0, 625, jnp.int32)
        _d = jax.random.randint(jax.random.fold_in(_gk, 3), (10000,), 0, 625, jnp.int32)
        _loop = jnp.arange(625, dtype=jnp.int32)
        src = jnp.concatenate([_s, _d, _loop])
        dst = jnp.concatenate([_d, _s, _loop])
        _o = jnp.argsort(dst, stable=True)
        src = src[_o]
        dst = dst[_o]
        edge_attr_128 = 1.36993e-05 + 0.999972 * jax.random.normal(jax.random.fold_in(_gk, 12), (20625, 128), jnp.float32)
        return (x, src, dst, edge_attr_128)
    x, src, dst, edge_attr_128 = _rec_inputs()

    def _L0_gnn_setup():
        import jax, jax.numpy as jnp
        import numpy as np
        N_NODES = 625
        key = jax.random.key(seed)
        ks = jax.random.split(key, 12)
        H, R, E = (512, 128, 10000)
        s = lambda fan_in: 1.0 / np.sqrt(fan_in)
        return {'x': jax.random.normal(ks[0], (N_NODES, H), dtype=jnp.float32), 'edge_rbf': jax.random.normal(ks[1], (E, R), dtype=jnp.float32), 'We1': jax.random.uniform(ks[2], (R, H), jnp.float32, -s(R), s(R)), 'be1': jax.random.uniform(ks[3], (H,), jnp.float32, -s(R), s(R)), 'We2': jax.random.uniform(ks[4], (H, H), jnp.float32, -s(H), s(H)), 'be2': jax.random.uniform(ks[5], (H,), jnp.float32, -s(H), s(H)), 'Wn1': jax.random.uniform(ks[6], (H, H), jnp.float32, -s(H), s(H)), 'bn1': jax.random.uniform(ks[7], (H,), jnp.float32, -s(H), s(H)), 'Wn2': jax.random.uniform(ks[8], (H, H), jnp.float32, -s(H), s(H)), 'bn2': jax.random.uniform(ks[9], (H,), jnp.float32, -s(H), s(H)), 'edge_index': jax.random.randint(ks[10], (2, E), 0, N_NODES, dtype=jnp.int64)}
    _L0_gnn_all = _L0_gnn_setup()
    _L0_gnn_in = {k: v for k, v in _L0_gnn_all.items() if k in ('We1', 'be1', 'We2', 'be2', 'Wn1', 'bn1', 'Wn2', 'bn2')}
    del _L0_gnn_all

    def _L1_gnn_setup():
        import jax, jax.numpy as jnp
        import numpy as np

        def _mean_agg(h, src, dst, n):
            s = jax.ops.segment_sum(h[src], dst, num_segments=n)
            deg = jax.ops.segment_sum(jnp.ones((src.shape[0],), h.dtype), dst, num_segments=n)
            return s / jnp.maximum(deg, 1.0)[:, None]
        key = jax.random.key(seed)
        ks = jax.random.split(key, 7)
        N, E, D, H, L = (625, 10000, 512, 512, 3)
        sc = 1.0 / np.sqrt(D)
        return {'feat': jax.random.normal(ks[0], (N, D), jnp.float32), 'src': jax.random.randint(ks[1], (E,), 0, N, jnp.int32), 'dst': jax.random.randint(ks[2], (E,), 0, N, jnp.int32), 'W_init': jax.random.normal(ks[3], (H, D), jnp.float32) * sc, 'W_fwd': jax.random.normal(ks[4], (L, H, H), jnp.float32) * sc, 'W_bwd': jax.random.normal(ks[5], (L, H, H), jnp.float32) * sc, 'W_self': jax.random.normal(ks[6], (L, H, 3 * H), jnp.float32) * (1.0 / np.sqrt(3 * H))}
    _L1_gnn_all = _L1_gnn_setup()
    _L1_gnn_in = {k: v for k, v in _L1_gnn_all.items() if k in ('W_init', 'W_fwd', 'W_bwd', 'W_self')}
    del _L1_gnn_all

    def _L2_gnn_setup():
        import jax, jax.numpy as jnp
        import numpy as np
        N_NODES = 3125
        N_EDGES = 25000
        IN_DIM = 512
        OUT_DIM = 512
        key = jax.random.key(seed)
        k1, k2, k3, k4 = jax.random.split(key, 4)
        x = jax.random.normal(k1, (N_NODES, IN_DIM), dtype=jnp.float32)
        edge_index = jax.random.randint(k2, (2, N_EDGES), 0, N_NODES, dtype=jnp.int64)
        W = jax.random.normal(k3, (OUT_DIM, IN_DIM), dtype=jnp.float32) / np.sqrt(IN_DIM)
        b = jax.random.normal(k4, (OUT_DIM,), dtype=jnp.float32) * 0.01
        return {'x': x, 'edge_index': edge_index, 'W': W, 'b': b}
    _L2_gnn_all = _L2_gnn_setup()
    _L2_gnn_in = {k: v for k, v in _L2_gnn_all.items() if k in ('W', 'b')}
    del _L2_gnn_all

    def _L3_gnn_setup():
        import jax, jax.numpy as jnp
        import numpy as np
        N_NODES = 6250
        N_EDGES = 18750

        def _gcn_conv(x, W, b, src, dst, n):
            h = x @ W
            loop = jnp.arange(n, dtype=src.dtype)
            s = jnp.concatenate([src, loop])
            d = jnp.concatenate([dst, loop])
            deg = jax.ops.segment_sum(jnp.ones(s.shape[0], dtype=x.dtype), d, num_segments=n)
            dinv = jnp.where(deg > 0, jax.lax.rsqrt(deg), jnp.zeros_like(deg))
            norm = dinv[s] * dinv[d]
            out = jax.ops.segment_sum(h[s] * norm[:, None], d, num_segments=n)
            return out + b
        key = jax.random.key(seed)
        ks = jax.random.split(key, 10)
        x = jax.random.normal(ks[0], (N_NODES, 512), dtype=jnp.float32)
        edge_index = jax.random.randint(ks[1], (2, N_EDGES), 0, N_NODES, dtype=jnp.int32)

        def lin(k, fan_in, fan_out):
            s = 1.0 / np.sqrt(fan_in)
            return jax.random.uniform(k, (fan_in, fan_out), jnp.float32, -s, s)
        W1 = lin(ks[2], 512, 256)
        b1 = jnp.zeros((256,), jnp.float32)
        W2 = lin(ks[3], 256, 128)
        b2 = jnp.zeros((128,), jnp.float32)
        W3 = lin(ks[4], 128, 128)
        b3 = jnp.zeros((128,), jnp.float32)
        s4 = 1.0 / np.sqrt(512)
        W4 = jax.random.uniform(ks[5], (512, 512), jnp.float32, -s4, s4)
        b4 = jax.random.uniform(ks[6], (512,), jnp.float32, -s4, s4)
        return {'x': x, 'W1': W1, 'b1': b1, 'W2': W2, 'b2': b2, 'W3': W3, 'b3': b3, 'W4': W4, 'b4': b4, 'edge_index': edge_index}
    _L3_gnn_all = _L3_gnn_setup()
    _L3_gnn_in = {k: v for k, v in _L3_gnn_all.items() if k in ('W1', 'b1', 'W2', 'b2', 'W3', 'b3', 'W4', 'b4')}
    del _L3_gnn_all
    return {'x': x, 'src': src, 'dst': dst, 'edge_attr_128': edge_attr_128, 'L0_gnn_We1': _L0_gnn_in['We1'], 'L0_gnn_be1': _L0_gnn_in['be1'], 'L0_gnn_We2': _L0_gnn_in['We2'], 'L0_gnn_be2': _L0_gnn_in['be2'], 'L0_gnn_Wn1': _L0_gnn_in['Wn1'], 'L0_gnn_bn1': _L0_gnn_in['bn1'], 'L0_gnn_Wn2': _L0_gnn_in['Wn2'], 'L0_gnn_bn2': _L0_gnn_in['bn2'], 'L1_gnn_W_init': _L1_gnn_in['W_init'], 'L1_gnn_W_fwd': _L1_gnn_in['W_fwd'], 'L1_gnn_W_bwd': _L1_gnn_in['W_bwd'], 'L1_gnn_W_self': _L1_gnn_in['W_self'], 'L2_gnn_W': _L2_gnn_in['W'], 'L2_gnn_b': _L2_gnn_in['b'], 'L3_gnn_W1': _L3_gnn_in['W1'], 'L3_gnn_b1': _L3_gnn_in['b1'], 'L3_gnn_W2': _L3_gnn_in['W2'], 'L3_gnn_b2': _L3_gnn_in['b2'], 'L3_gnn_W3': _L3_gnn_in['W3'], 'L3_gnn_b3': _L3_gnn_in['b3'], 'L3_gnn_W4': _L3_gnn_in['W4'], 'L3_gnn_b4': _L3_gnn_in['b4']}

def reference(x, src, dst, edge_attr_128, L0_gnn_We1, L0_gnn_be1, L0_gnn_We2, L0_gnn_be2, L0_gnn_Wn1, L0_gnn_bn1, L0_gnn_Wn2, L0_gnn_bn2, L1_gnn_W_init, L1_gnn_W_fwd, L1_gnn_W_bwd, L1_gnn_W_self, L2_gnn_W, L2_gnn_b, L3_gnn_W1, L3_gnn_b1, L3_gnn_W2, L3_gnn_b2, L3_gnn_W3, L3_gnn_b3, L3_gnn_W4, L3_gnn_b4):
    import jax
    import jax.numpy as jnp

    def _L0_gnn_ref(x, edge_rbf, We1, be1, We2, be2, Wn1, bn1, Wn2, bn2, edge_index):
        import jax, jax.numpy as jnp
        import numpy as np
        N_NODES = 625
        row, col = (edge_index[0], edge_index[1])
        edge_feature = jax.nn.silu(edge_rbf @ We1 + be1) @ We2 + be2
        msg = edge_feature * x[col]
        agg = jax.ops.segment_sum(msg, row, num_segments=N_NODES)
        return x + (jax.nn.silu(agg @ Wn1 + bn1) @ Wn2 + bn2)

    def _L1_gnn_ref(feat, src, dst, W_init, W_fwd, W_bwd, W_self):
        import jax, jax.numpy as jnp
        import numpy as np

        def _mean_agg(h, src, dst, n):
            s = jax.ops.segment_sum(h[src], dst, num_segments=n)
            deg = jax.ops.segment_sum(jnp.ones((src.shape[0],), h.dtype), dst, num_segments=n)
            return s / jnp.maximum(deg, 1.0)[:, None]
        n = feat.shape[0]
        h = jax.nn.relu(feat @ W_init.T)
        num_layers = W_fwd.shape[0]
        for l in range(num_layers):
            h_self = h
            fwd_neigh = _mean_agg(h, src, dst, n) @ W_fwd[l].T
            bwd_neigh = _mean_agg(h, dst, src, n) @ W_bwd[l].T
            cat = jnp.concatenate((h_self, fwd_neigh, bwd_neigh), axis=1)
            h = jax.nn.relu(cat @ W_self[l].T)
        return h

    def _L2_gnn_ref(x, edge_index, W, b):
        import jax, jax.numpy as jnp
        import numpy as np
        N_NODES = 3125
        N_EDGES = 25000
        IN_DIM = 512
        OUT_DIM = 512
        n = x.shape[0]
        loops = jnp.arange(n, dtype=edge_index.dtype)
        row = jnp.concatenate([edge_index[0], loops])
        col = jnp.concatenate([edge_index[1], loops])
        deg = jax.ops.segment_sum(jnp.ones(row.shape[0], dtype=x.dtype), row, num_segments=n)
        dis = jax.lax.rsqrt(deg)
        norm = dis[row] * dis[col]
        h = x @ W.T + b
        out = jax.ops.segment_sum(norm[:, None] * h[row], col, num_segments=n)
        return jax.nn.relu(out)

    def _L3_gnn_ref(x, W1, b1, W2, b2, W3, b3, W4, b4, edge_index):
        import jax, jax.numpy as jnp
        import numpy as np
        N_NODES = 6250
        N_EDGES = 18750

        def _gcn_conv(x, W, b, src, dst, n):
            h = x @ W
            loop = jnp.arange(n, dtype=src.dtype)
            s = jnp.concatenate([src, loop])
            d = jnp.concatenate([dst, loop])
            deg = jax.ops.segment_sum(jnp.ones(s.shape[0], dtype=x.dtype), d, num_segments=n)
            dinv = jnp.where(deg > 0, jax.lax.rsqrt(deg), jnp.zeros_like(deg))
            norm = dinv[s] * dinv[d]
            out = jax.ops.segment_sum(h[s] * norm[:, None], d, num_segments=n)
            return out + b
        n = x.shape[0]
        src, dst = (edge_index[0], edge_index[1])
        x1 = jax.nn.relu(_gcn_conv(x, W1, b1, src, dst, n))
        x2 = jax.nn.relu(_gcn_conv(x1, W2, b2, src, dst, n))
        x3 = jax.nn.relu(_gcn_conv(x2, W3, b3, src, dst, n))
        xc = jnp.concatenate([x1, x2, x3], axis=1)
        return xc @ W4.T + b4
    edge_index = jnp.stack([src, dst])
    h = jnp.maximum(_layernorm(x, axis=-1), 0.0)
    x = x + _L0_gnn_ref(h, edge_attr_128, L0_gnn_We1, L0_gnn_be1, L0_gnn_We2, L0_gnn_be2, L0_gnn_Wn1, L0_gnn_bn1, L0_gnn_Wn2, L0_gnn_bn2, edge_index)
    h = jnp.maximum(_layernorm(x, axis=-1), 0.0)
    x = x + _L1_gnn_ref(h, src, dst, L1_gnn_W_init, L1_gnn_W_fwd, L1_gnn_W_bwd, L1_gnn_W_self)
    h = jnp.maximum(_layernorm(x, axis=-1), 0.0)
    x = x + _L2_gnn_ref(h, edge_index, L2_gnn_W, L2_gnn_b)
    h = jnp.maximum(_layernorm(x, axis=-1), 0.0)
    x = x + _L3_gnn_ref(h, L3_gnn_W1, L3_gnn_b1, L3_gnn_W2, L3_gnn_b2, L3_gnn_W3, L3_gnn_b3, L3_gnn_W4, L3_gnn_b4, edge_index)
    return x

_drawn_inputs = setup_inputs


def setup_inputs(seed=0):
    import zlib

    import numpy as np

    out = dict(_drawn_inputs(seed))
    spreads = {'L3_gnn_b1': (0.0, 0.534), 'L3_gnn_b2': (0.0, 0.8), 'L3_gnn_b3': (0.0, 0.8)}
    factors = {'L0_gnn_be1': 2.707,
     'L0_gnn_bn1': 8.0,
     'L0_gnn_bn2': 3.695,
     'L2_gnn_b': 8.0,
     'L3_gnn_W2': 4.982,
     'L3_gnn_W3': 8.0,
     'L3_gnn_b4': 3.73}
    for name, (base, spread) in spreads.items():
        noise = np.random.default_rng([zlib.crc32(name.encode()), seed]).standard_normal(out[name].shape)
        drawn = base * np.exp(spread * noise) if base else spread * noise
        out[name] = jnp.asarray(drawn.astype(out[name].dtype))
    for name, factor in factors.items():
        out[name] = (out[name] * factor).astype(out[name].dtype)
    return out
```

```python
from contextlib import ExitStack

import concourse.bass as bass
from concourse import mybir

F32 = mybir.dt.float32
F32R = mybir.dt.float32r
BF16 = mybir.dt.bfloat16
F16 = mybir.dt.float16
I32 = mybir.dt.int32
ALU = mybir.AluOpType
ACT = mybir.ActivationFunctionType
AX = mybir.AxisListType.X

P = 128
N = 625
C = 5
NC = N // C
NP = N + 1
HALF = (314, 312)
F = 512
K = F // P
E = 20625
R = 128
EP = 125
ET = E // EP
PAIR = 2 * P
STEPS = (E + C * (PAIR - 1)) // PAIR
TILES = 2 * STEPS
FOLDS = 6
LAYERS = 3
W1C, W2C, W3C = 256, 128, 128

UNITS = [("aggT", 5, 5), ("mlp1", 8, 16), ("mlp2", 5, 0), ("adjT", 10, 11), ("h1T", 5, 5), ("init", 5, 5),
         ("initT", 10, 5), ("degrow", 4, 0), ("layer0", 31, 26), ("layer1", 31, 26), ("layer2", 21, 16),
         ("h2T", 5, 5), ("lin2", 5, 5), ("conv2", 5, 0), ("sumrow", 2, 2), ("h3T", 5, 5), ("lin_a", 5, 5),
         ("conv_a", 4, 8), ("lin_b", 5, 5), ("conv_b", 2, 4), ("lin_c", 5, 5), ("conv_c", 2, 4), ("last", 5, 0)]
UNIT, ACTS = {}, {}
_u = _a = 0
for _name, _units, _acts in UNITS:
    UNIT[_name], ACTS[_name] = _u, _a
    _u, _a = _u + _units, _a + _acts
LAYER_UNITS, LAYER_ACTS = 31, 26
NC_BYTES = C * F * 4
EPS = 1e-5


def each(eng, n, body):
    body(0)
    with eng.Fori(1, n) as m:
        body(m)


def wait_rounds(eng, sem, m, per, add=0):
    if not isinstance(m, int) or m * per + add > 0:
        eng.wait_ge(sem, m * per + add)


class Step:

    def __init__(self, reg, c):
        self.reg, self.c = reg, c

    def at(self, k):
        return Step(self.reg, self.c + k)

    @property
    def slot(self):
        return self.c % 2

    def count(self, per, add=0):
        if self.reg is None:
            return per * self.c + add
        return self.reg * (2 * per) + (per * self.c + add)

    def rounds(self, per):
        if self.reg is None:
            return per * (self.c // 2 + 1)
        return self.reg * per + per * (self.c // 2 + 1)

    def wait(self, eng, sem, per, add=0):
        if self.reg is not None or per * self.c + add > 0:
            eng.wait_ge(sem, self.count(per, add))


def steps(eng, n, body):
    pairs = (n - 5) // 2
    body(Step(None, 0))
    body(Step(None, 1))
    with eng.Fori(0, pairs) as i:
        body(Step(i, 2))
        body(Step(i, 3))
    for c in range(2 + 2 * pairs, n):
        body(Step(None, c))



def build(nc, a, out):
    with ExitStack() as ctx:
        def sem(name):
            return ctx.enter_context(nc.semaphore(name))

        base = (nc.sbuf_base + 63) // 64 * 64
        end = nc.sbuf_usable_end
        ctx.enter_context(nc.sbuf_tensor("arena", [P, end - base - 64], mybir.dt.uint8))
        size = {F32: 4, F32R: 4, I32: 4, BF16: 2, F16: 2}

        class Region:
            def __init__(self, at):
                self.at = at

            def __call__(self, name, shape, dt):
                n = size[dt]
                for s in shape[1:]:
                    n *= s
                t = nc.alloc_sbuf_tensor_at(name, shape, dt, offset=self.at)
                self.at += (n + 31) // 32 * 32
                assert self.at <= end, (name, self.at, end)
                return t

        keep = Region(base)
        x_res = keep("x_res", [NC, C, F], F32)
        part_col = keep("part_col", [NC, 3, C], F32)
        deg_col = keep("deg_col", [NC, 2, C], F32)
        root_col = keep("root_col", [NC, 2, C], F32)
        dinv_col = keep("dinv_col", [NC, 2, C], F32)
        ident = keep("ident", [P, P], F32)
        ones = keep("ones", [P, P], F32R)
        eps_col = keep("eps_col", [P, 1], F32)
        stats = keep("stats", [NC, C, 6], F32)
        mv = keep("mv", [NC, C, 2], F32)
        std = keep("std", [NC, C], F32)
        rstd = keep("rstd", [NC, C], F32)
        shift = keep("shift", [NC, C], F32)
        be1 = keep("be1", [P, K], F32)
        bn1 = keep("bn1", [P, K], F32)
        conv_bias = keep("conv_bias", [P, 4], F32)
        row_a = keep("row_a", [P, F], F32)
        row_b = keep("row_b", [P, F], F32)
        w_hi = [keep(f"w_hi{i}", [P, K, F], F32R) for i in range(3)]
        w_lo = [keep(f"w_lo{i}", [P, K, F], F32R) for i in range(3)]

        edge = Region(keep.at)
        acc_agg = edge("acc_agg", [NC, C * F], F32)
        acc_adj = edge("acc_adj", [NC, C * NP], F32)
        h32 = edge("h32", [NC, C, F], F32)
        h32_at = edge.at - NC_BYTES
        main = Region(edge.at)
        we1_hi = main("we1_hi", [P, F], F32R)
        we1_lo = main("we1_lo", [P, F], F32R)
        we2_hi = main("we2_hi", [P, K, F], F32R)
        we2_lo = main("we2_lo", [P, K, F], F32R)
        table = main("table", [P, TILES, 4], I32)
        bucket_row = main("bucket_row", [1, STEPS], I32)
        srccol = main("srccol", [P, TILES], F32)
        dstcol = main("dstcol", [P, TILES], F32)
        iota_s = main("iota_s", [P, NC + 1], F32)
        iota_d = main("iota_d", [P, NP], F16)
        loop = Region(main.at)
        edge_picks = [loop(f"edge_picks{i}", [P, 2], I32) for i in range(2)]
        node_picks = [loop(f"node_picks{i}", [P, 2], I32) for i in range(2)]
        rbf = [loop(f"rbf{i}", [P, 2, R], F32) for i in range(2)]
        xg = [loop(f"xg{i}", [P, 2, F], F32) for i in range(2)]
        rT_hi = [loop(f"rT_hi{i}", [P, PAIR], F32R) for i in range(2)]
        rT_lo = [loop(f"rT_lo{i}", [P, PAIR], F32R) for i in range(2)]
        s32 = loop("s32", [P, K, PAIR], F32)
        s_hi = [loop(f"s_hi{i}", [P, K, PAIR], F32R) for i in range(2)]
        s_lo = [loop(f"s_lo{i}", [P, K, PAIR], F32R) for i in range(2)]
        feat = [loop(f"feat{j}", [P, F], F32) for j in range(2)]
        msg = [loop(f"msg{j}", [P, F], F32) for j in range(2)]
        m_hi = [loop(f"m_hi{i}", [P, 2, F], F32R) for i in range(2)]
        m_lo = [loop(f"m_lo{i}", [P, 2, F], F32R) for i in range(2)]
        oh_src = [loop(f"oh_src{i}", [P, 2, NC + 1], F32R) for i in range(2)]
        oh_srcb = [loop(f"oh_srcb{i}", [P, 2, NC + 1], BF16) for i in range(2)]
        oh_dst = [loop(f"oh_dst{i}", [P, 2, NP], BF16) for i in range(2)]

        pre = Region(main.at)
        stage = pre("stage", [P, 2, K, F], F32)
        fold_hi = pre("fold_hi", [P, 2, K, F], F32R)
        fold_lo = pre("fold_lo", [P, 2, K, F], F32R)
        folded = pre("folded", [P, K, F], F32)
        src_i = pre("src_i", [EP, ET], I32)
        dst_i = pre("dst_i", [EP, ET], I32)
        src_f = pre("src_f", [EP, ET], F32)
        reach = pre("reach", [EP, C + 1, ET], F32)
        member = pre("member", [EP, C, ET], F32)
        rank = pre("rank", [EP, C, ET], F32)
        zeros = pre("zeros", [EP, ET], F32)
        place = pre("place", [EP, C, ET], F32)
        bucket = pre("bucket", [EP, ET], F32)
        pos_f = pre("pos_f", [EP, ET], F32)
        pos_i = pre("pos_i", [EP, ET], I32)
        pos_lo = pre("pos_lo", [EP, ET], I32)
        pos_hi = pre("pos_hi", [EP, ET], I32)
        row_i = pre("row_i", [EP, ET], I32)
        fields = pre("fields", [EP, ET, 4], I32)
        row_ring = pre("row_ring", [EP, 5], I32)
        field_ring = pre("field_ring", [EP, 5, 4], I32)
        empty = pre("empty", [P, TILES * 4], I32)
        before = pre("before", [P, P], F32)
        ones32 = pre("ones32", [P, P], F32)
        counts32 = pre("counts32", [EP, C], F32)
        total_i = pre("total_i", [EP, C], I32)
        chunks_i = pre("chunks_i", [EP, C], I32)
        chunks_f = pre("chunks_f", [EP, C], F32)
        upto = pre("upto", [EP, C], F32)
        first = pre("first", [EP, C], F32)
        offset = pre("offset", [EP, C], F32)
        step_row = pre("step_row", [1, STEPS], F32)
        bucket_f = [pre(f"bucket_f{i}", [1, STEPS], F32) for i in range(2)]

        node = Region(keep.at)
        z_hi = [None, None]
        z_lo = [None, None]
        z_hi[0] = node("zf_hi", [P, K, NP], F32R)
        z_lo[0] = node("zf_lo", [P, K, NP], F32R)
        z_hi[1] = node("zb_hi", [P, K, NP], F32R)
        z_lo[1] = node("zb_lo", [P, K, NP], F32R)
        adj_hi = [None, None]
        adj_lo = [None, None]
        adj_hi[0] = node("adj_hi", [NC, C, NP], F32R)
        adj_lo[0] = node("adj_lo", [NC, C, NP], F32R)
        adj_hi[1] = node("adjT_hi", [NC, C, NP], F32R)
        adj_lo[1] = node("adjT_lo", [NC, C, NP], F32R)
        share = Region(node.at)
        s1_hi = share("s1_hi", [P, K, NP], F32R)
        s1_lo = share("s1_lo", [P, K, NP], F32R)
        h_hi = node("h_hi", [NC, C, F], F32R)
        h_lo = node("h_lo", [NC, C, F], F32R)
        ht_hi = node("ht_hi", [P, K, NP], F32R)
        ht_lo = node("ht_lo", [P, K, NP], F32R)
        z32 = node("z32", [P, 2, HALF[0]], F32)
        rdeg = [node("rdeg_in", [P, NP], F32), node("rdeg_out", [P, NP], F32)]
        diag = Region(node.at)("diag", [NC, 2, C, NC], F32)
        wstage = node("wstage", [P, K * F], F32)
        late = Region(keep.at)
        relu32 = late("relu32", [P, 2, HALF[0]], F32)
        g32 = late("g32", [NC, C, F], F32)
        deg_row = late("deg_row", [P, NP], F32)
        root_row = late("root_row", [P, NP], F32)
        dinv_row = late("dinv_row", [P, NP], F32)
        assert late.at <= h32_at
        acc3 = acc_adj[:, :].rearrange("p (c n) -> p c n", c=C)
        agg3 = acc_agg[:, :].rearrange("p (c n) -> p c n", c=C)

        ps = ctx.enter_context(nc.psum_tensor("ps", [P, 8, 512], F32))

        h_dram = nc.dram_tensor("h_dram", [N, F], F32, kind="Internal").ap()
        slots_dram = nc.dram_tensor("slots_dram", [P * TILES, 4], I32, kind="Internal").ap()
        fold_dram = nc.dram_tensor("fold_dram", [FOLDS, P, K * F], F32, kind="Internal").ap()

        x_in, edges_in, small_in, h_saved = sem("x_in"), sem("edges_in"), sem("small_in"), sem("h_saved")
        consts_ready = sem("consts_ready")
        ln_stats, ln_act, ln_coef = sem("ln_stats"), sem("ln_act"), sem("ln_coef")
        res_ready = sem("res_ready")
        stage_in, split_hi, split_lo = sem("stage_in"), sem("split_hi"), sem("split_lo")
        fold_mm, fold_ev, fold_st = sem("fold_mm"), sem("fold_ev"), sem("fold_st")
        sort_step, rank_mm = sem("sort_step"), sem("rank_mm")
        empty_saved, ring_filled, table_in, cols_ready = (
            sem("empty_saved"), sem("ring_filled"), sem("table_in"), sem("cols_ready"))
        scattered = [sem(f"scattered{j}") for j in range(5)]
        picked = sem("picked")
        rbf_in = [sem(f"rbf_in{i}") for i in range(2)]
        xg_in = [sem(f"xg_in{i}") for i in range(2)]
        rT_mm, rT_hi_ready, rT_lo_ready = sem("rT_mm"), sem("rT_hi_ready"), sem("rT_lo_ready")
        z1_mm, silu_ready, s_hi_ready, s_lo_ready = sem("z1_mm"), sem("silu_ready"), sem("s_hi_ready"), sem("s_lo_ready")
        feat_mm, feat_ready, msg_ready = sem("feat_mm"), sem("feat_ready"), sem("msg_ready")
        m_hi_ready, m_lo_ready = sem("m_hi_ready"), sem("m_lo_ready")
        hots_ready, scat_mm, flushed = sem("hots_ready"), sem("scat_mm"), sem("flushed")
        filled, freed, act_done = sem("filled"), sem("freed"), sem("act_done")
        wstage_in, w_split, pads_ready = sem("wstage_in"), sem("w_split"), sem("pads_ready")
        adj_split, adj_self = sem("adj_split"), sem("adj_self")
        deg_step, deg_root, scaled = sem("deg_step"), sem("deg_root"), sem("scaled")
        rdeg_ready, scaled_x, rows_part = sem("rdeg_ready"), sem("scaled_x"), sem("rows_part")
        counts_ready, ranks_read = sem("counts_ready"), sem("ranks_read")
        z_lo_ready, split_g = sem("z_lo_ready"), sem("split_g")
        bias2_in, bias4_in, out_saved = sem("bias2_in"), sem("bias4_in"), sem("out_saved")

        block = ctx.enter_context(nc.Block())

        @block.sync
        def _(sp):
            sp.dma_start(src_i[:], a["src"]).then_inc(edges_in, 16)
            sp.dma_start(dst_i[:], a["dst"]).then_inc(edges_in, 16)
            sp.dma_start(x_res[:], a["x"].rearrange("(c p) f -> p c f", p=NC)).then_inc(x_in, 16)
            sp.dma_start(be1[:], a["be1"]).then_inc(small_in, 16)
            sp.dma_start(bn1[:], a["bn1"]).then_inc(small_in, 16)
            sp.dma_start(conv_bias[:], a["conv_bias"]).then_inc(small_in, 16)
            sp.dma_start(row_a[:], a["be2"].to_broadcast([P, F])).then_inc(small_in, 16)
            sp.dma_start(row_b[:], a["bn2"].to_broadcast([P, F])).then_inc(small_in, 16)
            sp.wait_ge(consts_ready, 1)
            sp.dma_start(slots_dram.rearrange("(p t) w -> p (t w)", p=P), empty[:]).then_inc(empty_saved, 16)
            sp.wait_ge(ln_act, 1 + C)
            sp.dma_start(h_dram.rearrange("(c p) f -> p c f", p=NC), h32[:]).then_inc(h_saved, 16)

            def load_factors(m):
                wait_rounds(sp, split_lo, m, 1)
                for part, w in enumerate((a["fold_a"], a["fold_b"])):
                    sp.dma_start(stage[:, part], w[bass.ds(m, 1)].rearrange("m p (k f) -> p (m k) f", k=K)).then_inc(stage_in, 16)

            def save_product(m):
                sp.wait_ge(fold_ev, (m + 1) * K)
                sp.dma_start(fold_dram[bass.ds(m, 1)].rearrange("m p f -> p (m f)"),
                             folded[:].rearrange("p k f -> p (k f)")).then_inc(fold_st, 16)

            load_factors(0)
            with sp.Fori(1, FOLDS) as m:
                load_factors(m)
                save_product(m - 1)
            sp.wait_ge(split_lo, FOLDS)
            sp.dma_start(stage[:, 0].rearrange("p k f -> p (k f)"), a["we2"]).then_inc(stage_in, 16)
            sp.dma_start(stage[:, 1, 0], a["we1"]).then_inc(stage_in, 16)
            save_product(FOLDS - 1)
            sp.wait_ge(split_lo, FOLDS + 2)
            sp.dma_start(stage[:, 0].rearrange("p k f -> p (k f)"), a["nodew"][0]).then_inc(stage_in, 16)
            sp.dma_start(stage[:, 1].rearrange("p k f -> p (k f)"), a["nodew"][1]).then_inc(stage_in, 16)
            sp.wait_ge(split_lo, FOLDS + 4)
            sp.dma_start(stage[:, 0].rearrange("p k f -> p (k f)"), a["nodew"][2]).then_inc(stage_in, 16)

            for j in range(5):
                sp.wait_ge(scattered[j], 16 * (ET // 5))
            sp.dma_start(table[:], slots_dram.rearrange("(p t) w -> p t w", p=P)).then_inc(table_in, 16)

            sp.wait_ge(flushed, 2 * STEPS)
            sp.wait_ge(fold_st, 16 * FOLDS)
            sources = []
            for l in range(LAYERS):
                sources += [a["selfw"][l], fold_dram[2 * l], fold_dram[2 * l + 1]]
            sources += [a["lin2"], a["conv_w"], a["lastw"]]
            for j, source in enumerate(sources):
                if j == 0:
                    sp.wait_ge(filled, UNIT["aggT"] + 1)
                    sp.dma_start(row_a[:], a["b2"].to_broadcast([P, F])).then_inc(bias2_in, 16)
                if j:
                    sp.wait_ge(w_split, 2 * j)
                if j == 3 * LAYERS:
                    sp.wait_ge(adj_self, 3 * C + 1)
                sp.dma_start(wstage[:], source).then_inc(wstage_in, 16)
            sp.wait_ge(freed, UNIT["h1T"])
            sp.dma_start(row_b[:], a["b4"].to_broadcast([P, F])).then_inc(bias4_in, 16)
            out3 = out.rearrange("(c p) f -> c p f", p=NC)
            for c in range(C):
                sp.wait_ge(freed, UNIT["last"] + c + 1)
                sp.dma_start(out3[c], x_res[:, c]).then_inc(out_saved, 16)
            sp.wait_ge(out_saved, 16 * C)

        @block.gpsimd
        def _(pool):
            pool.memset(empty[:], 0).then_inc(consts_ready, 1)
            pool.memset(eps_col[:], EPS).then_inc(consts_ready, 1)
            pool.memset(zeros[:], 0.0).then_inc(consts_ready, 1)
            pool.memset(ones[:].bitcast(F32), 1.0).then_inc(consts_ready, 1)
            pool.memset(ones32[:], 1.0).then_inc(consts_ready, 1)
            pool.memset(ident[:], 0.0).then_inc(consts_ready, 1)
            pool.iota(fields[:, :, 0], pattern=[[1, ET]], base=0, channel_multiplier=ET).then_inc(consts_ready, 1)
            pool.iota(step_row[:], pattern=[[1, STEPS]], base=0, channel_multiplier=0,
                      allow_small_or_imprecise_dtypes=True).then_inc(consts_ready, 1)
            pool.iota(iota_s[:], pattern=[[1, NC + 1]], base=1, channel_multiplier=0,
                      allow_small_or_imprecise_dtypes=True).then_inc(consts_ready, 1)
            pool.iota(iota_d[:], pattern=[[1, NP]], base=0, channel_multiplier=0,
                      allow_small_or_imprecise_dtypes=True).then_inc(consts_ready, 1)
            pool.wait_ge(consts_ready, 10)
            pool.affine_select(out=ident[:], in_=ident[:], compare_op=ALU.not_equal, fill=1.0,
                               base=0, pattern=[[-1, P]], channel_multiplier=1).then_inc(consts_ready, 1)
            pool.affine_select(out=before[:], in_=ones32[:], compare_op=ALU.is_gt, fill=0.0,
                               base=0, pattern=[[1, P]], channel_multiplier=-1).then_inc(consts_ready, 1)
            pool.memset(acc_agg[:], 0.0).then_inc(consts_ready, 1)
            pool.memset(acc_adj[:], 0.0).then_inc(consts_ready, 1)

            pool.wait_ge(empty_saved, 16)
            pool.wait_ge(rows_part, 3 * C + 5)
            for t in range(ET):
                pool.indirect_dma_start(
                    slots_dram, bass.IndirectOffsetOnAxis(ap=row_i[:, t:t + 1], axis=0),
                    fields[:, t], None).then_inc(scattered[t % 5], 16)

            pool.wait_ge(table_in, 16)
            pool.wait_ge(h_saved, 16)

            def pick_edges(t):
                t.wait(pool, rT_mm, 1, -1)
                pool.tensor_copy(edge_picks[t.slot][:], table[:, bass.ds(t.count(2), 2), 0]).then_inc(picked, 1)

            def pick_nodes(t):
                t.wait(pool, msg_ready, 2, -2)
                pool.tensor_copy(node_picks[t.slot][:], table[:, bass.ds(t.count(2), 2), 2]).then_inc(picked, 1)

            def gather_edges(t):
                for j in range(2):
                    pool.indirect_dma_start(
                        rbf[t.slot][:, j], None, a["edge"],
                        bass.IndirectOffsetOnAxis(ap=edge_picks[t.slot][:, j:j + 1], axis=0)).then_inc(rbf_in[t.slot], 16)

            def gather_nodes(t):
                for j in range(2):
                    pool.indirect_dma_start(
                        xg[t.slot][:, j], None, h_dram,
                        bass.IndirectOffsetOnAxis(ap=node_picks[t.slot][:, j:j + 1], axis=0)).then_inc(xg_in[t.slot], 16)

            def silu_lo(t):
                s = t.slot
                pool.wait_ge(s_hi_ready, t.count(1, 1))
                t.wait(pool, feat_mm, 2, -2)
                pool.tensor_tensor(s_lo[s][:], s32[:], s_hi[s][:], op=ALU.subtract).then_inc(s_lo_ready, 1)

            pool.wait_ge(split_lo, FOLDS + 5)
            for c in range(2):
                pick_edges(Step(None, c))
            pick_nodes(Step(None, 0))
            pool.wait_ge(picked, 3)
            gather_edges(Step(None, 0))
            gather_edges(Step(None, 1))
            gather_nodes(Step(None, 0))
            pick_edges(Step(None, 2))
            pool.wait_ge(picked, 4)
            gather_edges(Step(None, 2))
            silu_lo(Step(None, 0))

            def edge_step(t):
                def within(k):
                    return t.reg is not None or t.c + k < STEPS

                if within(3):
                    pick_edges(t.at(3))
                if within(1):
                    pick_nodes(t.at(1))
                    pool.wait_ge(picked, t.count(2, 6) if within(3) else t.c + STEPS + 2)
                    silu_lo(t.at(1))
                if within(1):
                    gather_nodes(t.at(1))
                if within(3):
                    gather_edges(t.at(3))

            steps(pool, STEPS, edge_step)

            pool.wait_ge(flushed, 2 * STEPS)
            for m in (adj_hi[1], adj_lo[1], ht_hi, ht_lo):
                pool.memset(m[:, :, N:NP].bitcast(F32), 0.0).then_inc(pads_ready, 1)
            pool.wait_ge(act_done, ACTS["adjT"] + 1)
            pool.tensor_tensor(adj_lo[0][:], acc3, adj_hi[0][:], op=ALU.subtract).then_inc(adj_split, 1)
            layer_end = [UNIT[f"layer{l}"] + 16 + C for l in range(LAYERS)]
            free = [UNIT["mlp1"] + 8, UNIT["mlp2"] + C, UNIT["init"] + C]
            for l in range(LAYERS):
                free += [layer_end[l]] * 3

            def add_loops():
                pool.wait_ge(filled, UNIT["layer2"] + 16)
                for c in range(C):
                    d = slice(c * NC, c * NC + NC)
                    pool.tensor_tensor(diag[:, 0, c], adj_hi[0][:, c, d], adj_lo[0][:, c, d],
                                       op=ALU.add).then_inc(adj_self, 1)
                pool.wait_ge(adj_self, C)
                pool.tensor_tensor(diag[:, 1], diag[:, 0], ident[0:NC, None, 0:NC].to_broadcast([NC, C, NC]),
                                   op=ALU.add).then_inc(adj_self, 1)
                pool.wait_ge(adj_self, C + 1)
                for c in range(C):
                    d = slice(c * NC, c * NC + NC)
                    pool.tensor_copy(adj_hi[0][:, c, d], diag[:, 1, c]).then_inc(adj_self, 1)
                pool.wait_ge(adj_self, 2 * C + 1)
                for c in range(C):
                    d = slice(c * NC, c * NC + NC)
                    pool.tensor_tensor(adj_lo[0][:, c, d], diag[:, 1, c], adj_hi[0][:, c, d],
                                       op=ALU.subtract).then_inc(adj_self, 1)

            for j in range(3 * (LAYERS + 1)):
                if j == 3 * LAYERS:
                    pool.wait_ge(w_split, 2 * j)
                    add_loops()
                pool.wait_ge(wstage_in, 16 * (j + 1))
                pool.wait_ge(filled, free[j])
                pool.tensor_copy(w_hi[j % 3][:].rearrange("p k f -> p (k f)"), wstage[:]).then_inc(w_split, 1)
                pool.wait_ge(w_split, 2 * j + 1)
                pool.tensor_tensor(w_lo[j % 3][:].rearrange("p k f -> p (k f)"), wstage[:],
                                   w_hi[j % 3][:].rearrange("p k f -> p (k f)"), op=ALU.subtract).then_inc(w_split, 1)

        @block.scalar
        def _(act):
            act.wait_ge(consts_ready, 11)

            def norm(k):
                act.wait_ge(ln_stats, 2 * C * (k + 1))
                act.activation(std[:], mv[:, :, 1], ACT.Sqrt, bias=eps_col[0:NC, :]).then_inc(ln_act, 1)
                act.wait_ge(ln_coef, 2 * (k + 1))
                for c in range(C):
                    act.activation(h32[:, c], x_res[:, c], ACT.Relu, bias=shift[:, c:c + 1],
                                   scale=rstd[:, c:c + 1]).then_inc(ln_act, 1)

            norm(0)

            def fold(m):
                act.wait_ge(stage_in, (m + 1) * 32)
                wait_rounds(act, fold_mm, m, K)
                act.activation(fold_hi[:], stage[:], ACT.Copy).then_inc(split_hi, 1)
                for u in range(K):
                    if u == 0:
                        wait_rounds(act, fold_st, m, 16)
                    act.wait_ge(fold_mm, m * K + u + 1)
                    act.activation(folded[:, u], ps[:, 1 + u], ACT.Copy).then_inc(fold_ev, 1)

            each(act, FOLDS, fold)
            act.wait_ge(stage_in, 32 * (FOLDS + 1))
            act.activation(we2_hi[:], stage[:, 0], ACT.Copy).then_inc(split_hi, 1)
            act.activation(we1_hi[:], stage[:, 1, 0], ACT.Copy).then_inc(split_hi, 1)
            act.wait_ge(stage_in, 32 * (FOLDS + 2))
            act.activation(w_hi[0][:], stage[:, 0], ACT.Copy).then_inc(split_hi, 1)
            act.activation(w_hi[1][:], stage[:, 1], ACT.Copy).then_inc(split_hi, 1)
            act.wait_ge(stage_in, 32 * (FOLDS + 2) + 16)
            act.activation(w_hi[2][:], stage[:, 0], ACT.Copy).then_inc(split_hi, 1)

            def rows_hi(t):
                s = t.slot
                act.wait_ge(rT_mm, t.count(1, 1))
                t.wait(act, z1_mm, 2, -2)
                act.activation(rT_hi[s][:], ps[:, 0, 0:PAIR], ACT.Copy).then_inc(rT_hi_ready, 1)

            def silu(t):
                s = t.slot
                t.wait(act, s_lo_ready, 1)
                t.wait(act, s_hi_ready, 1)
                for u in range(K):
                    act.wait_ge(z1_mm, t.count(2, u // 2 + 1))
                    act.activation(s32[:, u], ps[:, 1 + u // 2, (u % 2) * PAIR:(u % 2) * PAIR + PAIR],
                                   ACT.Silu, bias=be1[:, u:u + 1]).then_inc(silu_ready, 1)
                act.wait_ge(silu_ready, t.count(K, K))
                t.wait(act, feat_mm, 2, -2)
                act.activation(s_hi[s][:], s32[:], ACT.Copy).then_inc(s_hi_ready, 1)

            def message_hi(t, j):
                s = t.slot
                act.wait_ge(msg_ready, t.count(2, j + 1))
                t.wait(act, scat_mm, 2, -2)
                act.activation(m_hi[s][:, j], msg[j][:], ACT.Copy).then_inc(m_hi_ready, 1)

            act.wait_ge(split_lo, FOLDS + 5)
            act.wait_ge(small_in, 80)
            rows_hi(Step(None, 0))
            silu(Step(None, 0))
            rows_hi(Step(None, 1))

            def edge_step(t):
                if t.reg is not None or t.c + 1 < STEPS:
                    silu(t.at(1))
                if t.reg is not None or t.c + 2 < STEPS:
                    rows_hi(t.at(2))
                message_hi(t, 0)
                message_hi(t, 1)

            steps(act, STEPS, edge_step)

            def copy_units(stage_name, n, view, func=ACT.Copy):
                for i in range(n):
                    act.wait_ge(filled, UNIT[stage_name] + i + 1)
                    dst, src = view(i)
                    act.activation(dst, src, func).then_inc(act_done, 1)

            def bank(u):
                return ps[:, u % 8]

            def turned(stage_name):
                return lambda c: (ht_hi[:, :, c * NC:c * NC + NC],
                                  bank(UNIT[stage_name] + c)[:, 0:K * NC].rearrange("p (k n) -> p k n", k=K))

            act.wait_ge(flushed, 2 * STEPS)
            copy_units("aggT", C, turned("aggT"))
            for i in range(2 * K):
                u = UNIT["mlp1"] + i
                g, half, w = i // 2, i % 2, HALF[i % 2]
                cols = slice(half * HALF[0], half * HALF[0] + w)
                act.wait_ge(filled, u + 1)
                if i >= 2:
                    act.wait_ge(freed, u - 1)
                act.activation(z32[:, i % 2, 0:w], bank(u)[:, 0:w], ACT.Silu, bias=bn1[:, g:g + 1]).then_inc(act_done, 1)
                act.wait_ge(act_done, ACTS["mlp1"] + 2 * i + 1)
                act.activation(s1_hi[:, g, cols], z32[:, i % 2, 0:w], ACT.Copy).then_inc(act_done, 1)
            act.activation(adj_hi[0][:], acc3, ACT.Copy).then_inc(act_done, 1)

            def adjT_hi(i):
                j, part = i // 2, i % 2
                cols = slice(0, 4 * NC) if part == 0 else slice(4 * NC, N)
                w = 4 * NC if part == 0 else NC
                return adj_hi[1][:, j, cols], bank(UNIT["adjT"] + i)[0:NC, 0:w]

            norm(1)
            copy_units("adjT", 2 * C, adjT_hi)
            copy_units("h1T", C, turned("h1T"))

            def node_rows(unit):
                return lambda c: (h_hi[:, c], bank(unit + c)[0:NC, :])

            copy_units("init", C, node_rows(UNIT["init"]), ACT.Relu)

            def turned_hi(unit, count):
                for c in range(C):
                    act.wait_ge(filled, count(2 * c + 1))
                    act.activation(ht_hi[:, :, c * NC:c * NC + NC],
                                   ps[:, (unit + 2 * c) % 8, 0:K * NC].rearrange("p (k n) -> p k n", k=K),
                                   ACT.Copy).then_inc(act_done, 1)

            turned_hi(UNIT["initT"], lambda n: UNIT["initT"] + n)

            def layer(l, last):
                def count(n):
                    return l * LAYER_UNITS + (UNIT["layer0"] + n)

                for i in range(16):
                    d, f, half, w = i // 8, i % 8 // 2, i % 2, HALF[i % 2]
                    cols = slice(half * HALF[0], half * HALF[0] + w)
                    act.wait_ge(freed, count(i + 1))
                    act.activation(z_hi[d][:, f, cols], z32[:, i % 2, 0:w], ACT.Copy).then_inc(act_done, 1)
                if last:
                    return
                for c in range(C):
                    act.wait_ge(filled, count(17 + c))
                    act.activation(h_hi[:, c], ps[0:NC, (16 + c) % 8], ACT.Relu).then_inc(act_done, 1)
                turned_hi(21, lambda n: count(21 + n))

            with act.Fori(0, LAYERS - 1) as l:
                layer(l, False)
            layer(LAYERS - 1, True)

            act.wait_ge(deg_step, 5)
            act.activation(root_col[:], deg_col[:], ACT.Sqrt).then_inc(deg_root, 1)
            norm(2)
            copy_units("h2T", C, turned("h2T"))
            for c in range(C):
                act.wait_ge(freed, UNIT["lin2"] + c + 1)
                act.activation(h_hi[:, c], g32[:, c], ACT.Copy, scale=dinv_col[:, 0, c:c + 1]).then_inc(act_done, 1)
            for half in range(2):
                act.wait_ge(freed, UNIT["sumrow"] + half + 1)
                cols = slice(half * HALF[0], half * HALF[0] + HALF[half])
                act.activation(root_row[:, cols], deg_row[:, cols], ACT.Sqrt).then_inc(act_done, 1)
            norm(3)
            copy_units("h3T", C, turned("h3T"))

            def conv(name, lin, f0, chunks):
                for c in range(C):
                    act.wait_ge(filled, UNIT[lin] + c + 1)
                    w = chunks * P
                    act.activation(h_hi[:, c, 0:w], bank(UNIT[lin] + c)[0:NC, 0:w], ACT.Copy,
                                   scale=dinv_col[:, 1, c:c + 1]).then_inc(act_done, 1)
                for i in range(2 * chunks):
                    u = UNIT[name] + i
                    f, half, w = f0 + i // 2, i % 2, HALF[i % 2]
                    cols = slice(half * HALF[0], half * HALF[0] + w)
                    act.wait_ge(scaled, 2 * (f0 + i // 2) + half + 1)
                    if i >= 2:
                        act.wait_ge(freed, u - 1)
                    act.activation(relu32[:, i % 2, 0:w], z32[:, i % 2, 0:w], ACT.Relu,
                                   bias=conv_bias[:, f:f + 1]).then_inc(act_done, 1)
                    act.wait_ge(act_done, ACTS[name] + 2 * i + 1)
                    act.activation(ht_hi[:, f, cols], relu32[:, i % 2, 0:w], ACT.Copy).then_inc(act_done, 1)

            conv("conv_a", "lin_a", 0, 2)
            conv("conv_b", "lin_b", 2, 1)
            conv("conv_c", "lin_c", 3, 1)

        @block.tensor
        def _(pe):
            def three(outp, left, right, start, stop):
                (lh, ll), (rh, rl) = left, right
                pe.matmul(outp, lh, rh, start=start, stop=False)
                pe.matmul(outp, lh, rl, start=False, stop=False)
                return pe.matmul(outp, ll, rh, start=False, stop=stop)

            pe.wait_ge(consts_ready, 12)
            pe.wait_ge(counts_ready, 1)
            pe.matmul(ps[0:EP, 0, 0:C], before[0:EP, 0:EP], counts32[:], start=True, stop=True).then_inc(rank_mm, 1)
            pe.matmul(ps[0:EP, 1, 0:C], ones32[0:EP, 0:EP], counts32[:], start=True, stop=True).then_inc(rank_mm, 1)
            pe.wait_ge(ranks_read, 1)

            def fold(m):
                pe.wait_ge(split_hi, m + 1)
                pe.wait_ge(split_lo, m + 1)
                for u in range(K):
                    wait_rounds(pe, fold_ev, m, K, u + 1 - K)
                    for k in range(K):
                        f = slice(u * P, u * P + P)
                        mm = three(ps[:, 1 + u], (fold_hi[:, 0, k, f], fold_lo[:, 0, k, f]),
                                   (fold_hi[:, 1, k], fold_lo[:, 1, k]), k == 0, k == K - 1)
                    mm.then_inc(fold_mm, 1)

            each(pe, FOLDS, fold)
            pe.wait_ge(fold_ev, K * FOLDS)

            def turn_rows(t):
                s = t.slot
                pe.wait_ge(rbf_in[s], t.rounds(32))
                t.wait(pe, rT_lo_ready, 1)
                pe.transpose(ps[:, 0, 0:P], rbf[s][:, 0], ident[:])
                pe.transpose(ps[:, 0, P:PAIR], rbf[s][:, 1], ident[:]).then_inc(rT_mm, 1)

            def first_layer(t):
                s = t.slot
                pe.wait_ge(rT_hi_ready, t.count(1, 1))
                pe.wait_ge(rT_lo_ready, t.count(1, 1))
                t.wait(pe, silu_ready, K)
                for u in range(K):
                    f = slice(u * P, u * P + P)
                    mm = three(ps[:, 1 + u // 2, (u % 2) * PAIR:(u % 2) * PAIR + PAIR],
                               (we1_hi[:, f], we1_lo[:, f]), (rT_hi[s][:], rT_lo[s][:]), True, True)
                    if u % 2:
                        mm.then_inc(z1_mm, 1)

            def second_layer(t, j):
                s = t.slot
                e = slice(j * P, j * P + P)
                pe.wait_ge(s_hi_ready, t.count(1, 1))
                pe.wait_ge(s_lo_ready, t.count(1, 1))
                t.wait(pe, feat_ready, 2, j - 1)
                for k in range(K):
                    mm = three(ps[:, 3 + j], (s_hi[s][:, k, e], s_lo[s][:, k, e]),
                               (we2_hi[:, k], we2_lo[:, k]), k == 0, k == K - 1)
                mm.then_inc(feat_mm, 1)

            def scatter(t):
                s = t.slot
                pe.wait_ge(m_hi_ready, t.count(2, 2))
                pe.wait_ge(m_lo_ready, t.count(2, 2))
                pe.wait_ge(hots_ready, t.count(6, 6))
                t.wait(pe, flushed, 2, -1)
                for j in range(2):
                    pe.matmul(ps[0:NC, 5], oh_src[s][:, j, 0:NC], m_hi[s][:, j], start=j == 0, stop=False)
                    mm = pe.matmul(ps[0:NC, 5], oh_src[s][:, j, 0:NC], m_lo[s][:, j], start=False, stop=j == 1)
                mm.then_inc(scat_mm, 1)
                t.wait(pe, flushed, 2)
                for j in range(2):
                    pe.matmul(ps[0:NC, 6], oh_srcb[s][:, j, 0:NC], oh_dst[s][:, j, 0:512], start=j == 0, stop=j == 1)
                for j in range(2):
                    mm = pe.matmul(ps[0:NC, 7, 0:NP - 512], oh_srcb[s][:, j, 0:NC], oh_dst[s][:, j, 512:NP],
                                   start=j == 0, stop=j == 1)
                mm.then_inc(scat_mm, 1)

            pe.wait_ge(split_hi, FOLDS + 2)
            pe.wait_ge(split_lo, FOLDS + 2)
            turn_rows(Step(None, 0))
            first_layer(Step(None, 0))
            turn_rows(Step(None, 1))

            def edge_step(t):
                if t.reg is not None or t.c + 1 < STEPS:
                    first_layer(t.at(1))
                second_layer(t, 0)
                if t.reg is not None or t.c + 2 < STEPS:
                    turn_rows(t.at(2))
                second_layer(t, 1)
                if t.reg is not None or t.c > 0:
                    scatter(t.at(-1))

            steps(pe, STEPS, edge_step)
            scatter(Step(None, STEPS - 1))

            def unit(u):
                if u >= 8:
                    pe.wait_ge(freed, u - 7)
                return ps[:, u % 8]

            def turn(stage_name, src, ready, *need):
                for c in range(C):
                    pe.wait_ge(ready, need[0] + c if len(need) == 1 else need[0])
                    b = unit(UNIT[stage_name] + c)
                    for k in range(K):
                        mm = pe.transpose(b[:, k * NC:k * NC + NC], src(c, k), ident[0:NC, 0:NC])
                    mm.then_inc(filled, 1)

            def halves(i):
                w = HALF[i % 2]
                return slice((i % 2) * HALF[0], (i % 2) * HALF[0] + w), w

            def ht(k, c):
                n = slice(c * NC, c * NC + NC)
                return ht_hi[:, k, n], ht_lo[:, k, n]

            def linear(stage_name, slot, width, at=0, ks=range(K)):
                ks = list(ks)
                hi = w_hi[slot][:].rearrange("p k f -> p (k f)")
                lo = w_lo[slot][:].rearrange("p k f -> p (k f)")
                for c in range(C):
                    b = unit(UNIT[stage_name] + c)
                    for n, k in enumerate(ks):
                        w = slice(at + n * width, at + n * width + width)
                        mm = three(b[0:NC, 0:width], ht(k, c), (hi[:, w], lo[:, w]), n == 0, n == len(ks) - 1)
                    mm.then_inc(filled, 1)

            pe.wait_ge(flushed, 2 * STEPS)
            turn("aggT", lambda c, k: agg3[:, c, k * P:k * P + P], flushed, 2 * STEPS, 0)
            pe.wait_ge(pads_ready, 4)
            pe.wait_ge(act_done, ACTS["aggT"] + C)
            pe.wait_ge(freed, UNIT["aggT"] + C)
            for i in range(2 * K):
                g = slice(i // 2 * P, i // 2 * P + P)
                cols, w = halves(i)
                b = unit(UNIT["mlp1"] + i)
                for k in range(K):
                    mm = three(b[:, 0:w], (w_hi[0][:, k, g], w_lo[0][:, k, g]),
                               (ht_hi[:, k, cols], ht_lo[:, k, cols]), k == 0, k == K - 1)
                mm.then_inc(filled, 1)
            pe.wait_ge(act_done, ACTS["mlp1"] + 4 * K)
            pe.wait_ge(freed, UNIT["mlp1"] + 2 * K)
            for c in range(C):
                n = slice(c * NC, c * NC + NC)
                b = unit(UNIT["mlp2"] + c)
                for k in range(K):
                    mm = three(b[0:NC], (s1_hi[:, k, n], s1_lo[:, k, n]), (w_hi[1][:, k], w_lo[1][:, k]),
                               k == 0, k == K - 1)
                mm.then_inc(filled, 1)

            for j in range(C):
                n = slice(j * NC, j * NC + NC)
                for part in range(2):
                    b = unit(UNIT["adjT"] + 2 * j + part)
                    for c in (range(4) if part == 0 else [4]):
                        at = c * NC if part == 0 else 0
                        mm = pe.transpose(b[0:NC, at:at + NC], acc3[:, c, n], ident[0:NC, 0:NC])
                    mm.then_inc(filled, 1)

            turn("h1T", lambda c, k: h32[:, c, k * P:k * P + P], ln_act, 2 * (1 + C) - C + 1)
            pe.wait_ge(act_done, ACTS["h1T"] + C)
            pe.wait_ge(freed, UNIT["h1T"] + C)
            linear("init", 2, F)

            def turn_split(count, unit_of):
                for c in range(C):
                    for part, src in enumerate((h_hi, h_lo)):
                        b = unit_of(2 * c + part)
                        for k in range(K):
                            mm = pe.transpose(b[:, k * NC:k * NC + NC],
                                              src[:, c, k * P:k * P + P].bitcast(F32), ident[0:NC, 0:NC])
                        mm.then_inc(filled, 1)

            pe.wait_ge(act_done, ACTS["init"] + C)
            pe.wait_ge(freed, UNIT["init"] + C)
            turn_split(None, lambda n: unit(UNIT["initT"] + n))

            pe.wait_ge(adj_split, 1)
            for d in range(2):
                for i in range(2):
                    cols, w = halves(i)
                    b = unit(UNIT["degrow"] + 2 * d + i)
                    for c in range(C):
                        pe.matmul(b[:, 0:w], ones[0:NC, :], adj_hi[d][:, c, cols], start=c == 0, stop=False)
                        mm = pe.matmul(b[:, 0:w], ones[0:NC, :], adj_lo[d][:, c, cols], start=False, stop=c == C - 1)
                    mm.then_inc(filled, 1)

            def layer(l, last):
                def count(n):
                    return l * LAYER_UNITS + (UNIT["layer0"] + n)

                def layer_unit(n):
                    pe.wait_ge(freed, count(n - 6 if n < 8 else n - 7))
                    return ps[:, n % 8]

                pe.wait_ge(freed, count(0))
                for i in range(16):
                    d, f = i // 8, i % 8 // 2
                    cols, w = halves(i)
                    b = layer_unit(i)
                    fs = slice(f * P, f * P + P)
                    for c in range(C):
                        mm = three(b[:, 0:w], (h_hi[:, c, fs], h_lo[:, c, fs]),
                                   (adj_hi[d][:, c, cols], adj_lo[d][:, c, cols]), c == 0, c == C - 1)
                    mm.then_inc(filled, 1)
                pe.wait_ge(w_split, (l + 1) * 6)
                for c in range(C):
                    b = layer_unit(16 + c)
                    n = slice(c * NC, c * NC + NC)
                    for m in range(3):
                        if c == 0 and m:
                            pe.wait_ge(z_lo_ready, l * 16 + 8 * m)
                        for k in range(K):
                            left = ht(k, c) if m == 0 else (z_hi[m - 1][:, k, n], z_lo[m - 1][:, k, n])
                            mm = three(b[0:NC], left, (w_hi[m][:, k], w_lo[m][:, k]),
                                       m == 0 and k == 0, m == 2 and k == K - 1)
                    mm.then_inc(filled, 1)
                if not last:
                    pe.wait_ge(freed, count(16 + C))
                    turn_split(None, lambda n: layer_unit(21 + n))

            with pe.Fori(0, LAYERS - 1) as l:
                layer(l, False)
            layer(LAYERS - 1, True)

            pe.wait_ge(freed, UNIT["h2T"])
            turn("h2T", lambda c, k: h32[:, c, k * P:k * P + P], ln_act, 3 * (1 + C) - C + 1)
            pe.wait_ge(act_done, ACTS["h2T"] + C)
            pe.wait_ge(freed, UNIT["h2T"] + C)
            pe.wait_ge(w_split, 2 * 3 * LAYERS + 2)
            linear("lin2", 0, F)
            pe.wait_ge(act_done, ACTS["lin2"] + C)
            pe.wait_ge(split_g, C)
            pe.wait_ge(adj_self, 3 * C + 1)
            for c in range(C):
                n = slice(c * NC, c * NC + NC)
                b = unit(UNIT["conv2"] + c)
                for q in range(C):
                    mm = three(b[0:NC], (adj_hi[0][:, q, n], adj_lo[0][:, q, n]), (h_hi[:, q], h_lo[:, q]),
                               q == 0, q == C - 1)
                mm.then_inc(filled, 1)
            for i in range(2):
                cols, w = halves(i)
                b = unit(UNIT["sumrow"] + i)
                for c in range(C):
                    pe.matmul(b[:, 0:w], ones[0:NC, :], adj_hi[0][:, c, cols], start=c == 0, stop=False)
                    mm = pe.matmul(b[:, 0:w], ones[0:NC, :], adj_lo[0][:, c, cols], start=False, stop=c == C - 1)
                mm.then_inc(filled, 1)

            turn("h3T", lambda c, k: h32[:, c, k * P:k * P + P], ln_act, 4 * (1 + C) - C + 1)
            pe.wait_ge(act_done, ACTS["h3T"] + C)
            pe.wait_ge(freed, UNIT["h3T"] + C)
            pe.wait_ge(w_split, 2 * 3 * LAYERS + 4)

            def conv(lin, name, f0, chunks):
                pe.wait_ge(act_done, ACTS[lin] + C)
                pe.wait_ge(freed, UNIT[lin] + C)
                for i in range(2 * chunks):
                    fs = slice(i // 2 * P, i // 2 * P + P)
                    cols, w = halves(i)
                    b = unit(UNIT[name] + i)
                    for c in range(C):
                        mm = three(b[:, 0:w], (h_hi[:, c, fs], h_lo[:, c, fs]),
                                   (adj_hi[0][:, c, cols], adj_lo[0][:, c, cols]), c == 0, c == C - 1)
                    mm.then_inc(filled, 1)
                pe.wait_ge(act_done, ACTS[name] + 4 * chunks)
                pe.wait_ge(freed, UNIT[name] + 2 * chunks)

            linear("lin_a", 1, W1C)
            conv("lin_a", "conv_a", 0, 2)
            linear("lin_b", 1, W2C, at=K * W1C, ks=(0, 1))
            conv("lin_b", "conv_b", 2, 1)
            linear("lin_c", 1, W3C, at=K * W1C + 2 * W2C, ks=(2,))
            conv("lin_c", "conv_c", 3, 1)
            pe.wait_ge(w_split, 2 * 3 * (LAYERS + 1))
            linear("last", 2, F)

        @block.vector
        def _(dve):
            def bank(u):
                return ps[:, u % 8]

            def norm(k, ready, need):
                for c in range(C):
                    dve.wait_ge(ready, need)
                    dve.bn_stats(stats[:, c], x_res[:, c]).then_inc(ln_stats, 1)
                dve.wait_ge(ln_stats, 2 * C * k + C)
                for c in range(C):
                    dve.bn_aggr(mv[:, c], stats[:, c]).then_inc(ln_stats, 1)
                dve.wait_ge(ln_act, (1 + C) * k + 1)
                dve.reciprocal(rstd[:], std[:]).then_inc(ln_coef, 1)
                dve.wait_ge(ln_coef, 2 * k + 1)
                dve.scalar_tensor_tensor(out=shift[:], in0=mv[:, :, 0], scalar=-1.0, in1=rstd[:],
                                         op0=ALU.mult, op1=ALU.mult).then_inc(ln_coef, 1)

            norm(0, x_in, 16)

            chain = [0]

            def link(ins):
                chain[0] += 1
                ins.then_inc(sort_step, 1)
                dve.wait_ge(sort_step, chain[0])

            dve.wait_ge(edges_in, 32)
            dve.wait_ge(consts_ready, 14)
            link(dve.tensor_copy(src_f[:], src_i[:]))
            dve.memset(reach[:, 0], 1.0).then_inc(rows_part, 1)
            dve.memset(reach[:, C], 0.0).then_inc(rows_part, 1)
            for b in range(1, C):
                dve.tensor_scalar(reach[:, b], src_f[:], float(b * NC), None, ALU.is_ge).then_inc(rows_part, 1)
            dve.wait_ge(rows_part, C + 1)
            link(dve.tensor_tensor(member[:], reach[:, 0:C], reach[:, 1:C + 1], op=ALU.subtract))
            for b in range(C):
                dve.tensor_tensor_scan(rank[:, b], member[:, b], zeros[:], 0.0, ALU.add, ALU.add).then_inc(rows_part, 1)
            dve.wait_ge(rows_part, 2 * C + 1)
            dve.tensor_copy(counts32[:], rank[:, :, ET - 1]).then_inc(counts_ready, 1)
            dve.wait_ge(rank_mm, 2)
            link(dve.tensor_scalar(total_i[:], ps[0:EP, 1, 0:C], float(PAIR - 1), None, ALU.add))
            shift_by = PAIR.bit_length() - 1
            link(dve.tensor_scalar(chunks_i[:], total_i[:], shift_by, None, ALU.logical_shift_right))
            link(dve.tensor_copy(chunks_f[:], chunks_i[:]))
            link(dve.tensor_tensor_scan(upto[:], chunks_f[:], zeros[:, 0:C], 0.0, ALU.add, ALU.add))
            link(dve.tensor_tensor(first[:], upto[:], chunks_f[:], op=ALU.subtract))
            link(dve.scalar_tensor_tensor(out=offset[:], in0=first[:], scalar=float(PAIR), in1=ps[0:EP, 0, 0:C],
                                          op0=ALU.mult, op1=ALU.add))
            dve.tensor_reduce(bucket[:], reach[:, 1:C].rearrange("p b t -> p t b"), axis=AX,
                              op=ALU.add).then_inc(ranks_read, 1)
            for b in range(C):
                dve.scalar_tensor_tensor(out=place[:, b], in0=rank[:, b], scalar=offset[:, b:b + 1],
                                         in1=member[:, b], op0=ALU.add, op1=ALU.mult).then_inc(rows_part, 1)
            dve.wait_ge(rows_part, 3 * C + 1)
            link(dve.tensor_reduce(pos_f[:], place[:].rearrange("p b t -> p t b"), axis=AX, op=ALU.add))
            link(dve.tensor_scalar(pos_i[:], pos_f[:], -1.0, None, ALU.add))
            link(dve.tensor_scalar(pos_lo[:], pos_i[:], P - 1, None, ALU.bitwise_and))
            link(dve.tensor_scalar(pos_hi[:], pos_i[:], P.bit_length() - 1, None, ALU.logical_shift_right))
            dve.scalar_tensor_tensor(out=row_i[:], in0=pos_lo[:], scalar=float(TILES), in1=pos_hi[:],
                                     op0=ALU.mult, op1=ALU.add).then_inc(rows_part, 1)
            dve.wait_ge(ranks_read, 1)
            link(dve.scalar_tensor_tensor(out=pos_f[:], in0=bucket[:], scalar=-float(NC), in1=src_f[:],
                                          op0=ALU.mult, op1=ALU.add))
            dve.tensor_scalar(fields[:, :, 1], pos_f[:], 1.0, None, ALU.add).then_inc(rows_part, 1)
            dve.tensor_copy(fields[:, :, 2], dst_i[:]).then_inc(rows_part, 1)
            dve.tensor_copy(fields[:, :, 3], dst_i[:]).then_inc(rows_part, 1)
            link(dve.tensor_scalar(bucket_f[0][:], step_row[:], first[0:1, 1:2], None, ALU.is_ge))
            for b in range(2, C):
                o = bucket_f[(b + 1) % 2] if b < C - 1 else bucket_row
                link(dve.scalar_tensor_tensor(out=o[:], in0=step_row[:], scalar=first[0:1, b:b + 1],
                                              in1=bucket_f[b % 2][:], op0=ALU.is_ge, op1=ALU.add))

            dve.wait_ge(small_in, 80)
            for c in range(C):
                dve.wait_ge(ln_act, 1 + C)
                dve.tensor_tensor(x_res[:, c], x_res[:, c], h32[:, c], op=ALU.add).then_inc(res_ready, 1)
            for c in range(C):
                dve.wait_ge(res_ready, c + 1)
                dve.tensor_tensor(x_res[:, c], x_res[:, c], row_b[0:NC], op=ALU.add).then_inc(res_ready, 1)

            def fold(m):
                dve.wait_ge(split_hi, m + 1)
                dve.tensor_tensor(fold_lo[:], stage[:], fold_hi[:], op=ALU.subtract).then_inc(split_lo, 1)

            each(dve, FOLDS, fold)
            dve.wait_ge(split_hi, FOLDS + 1)
            dve.tensor_tensor(we2_lo[:], stage[:, 0], we2_hi[:], op=ALU.subtract).then_inc(split_lo, 1)
            dve.wait_ge(split_hi, FOLDS + 2)
            dve.tensor_tensor(we1_lo[:], stage[:, 1, 0], we1_hi[:], op=ALU.subtract).then_inc(split_lo, 1)
            for i in range(3):
                dve.wait_ge(split_hi, FOLDS + 3 + i)
                dve.tensor_tensor(w_lo[i][:], stage[:, i % 2], w_hi[i][:], op=ALU.subtract).then_inc(split_lo, 1)
            dve.wait_ge(table_in, 16)
            dve.tensor_copy(srccol[:], table[:, :, 1]).then_inc(cols_ready, 1)
            dve.tensor_copy(dstcol[:], table[:, :, 2]).then_inc(cols_ready, 1)
            dve.wait_ge(cols_ready, 2)
            dve.wait_ge(split_lo, FOLDS + 5)

            def rows_lo(t):
                s = t.slot
                dve.wait_ge(rT_hi_ready, t.count(1, 1))
                dve.tensor_tensor(rT_lo[s][:], ps[:, 0, 0:PAIR], rT_hi[s][:], op=ALU.subtract).then_inc(rT_lo_ready, 1)

            def edge_feature(t, j):
                dve.wait_ge(feat_mm, t.count(2, j + 1))
                t.wait(dve, msg_ready, 2, j - 1)
                dve.tensor_tensor(feat[j][:], ps[:, 3 + j], row_a[:], op=ALU.add).then_inc(feat_ready, 1)

            def message(t, j):
                s = t.slot
                dve.wait_ge(feat_ready, t.count(2, j + 1))
                dve.wait_ge(xg_in[s], t.rounds(32))
                t.wait(dve, m_lo_ready, 2, j - 1)
                dve.tensor_tensor(msg[j][:], feat[j][:], xg[s][:, j], op=ALU.mult).then_inc(msg_ready, 1)

            def message_lo(t, j):
                s = t.slot
                dve.wait_ge(m_hi_ready, t.count(2, j + 1))
                dve.tensor_tensor(m_lo[s][:, j], msg[j][:], m_hi[s][:, j], op=ALU.subtract).then_inc(m_lo_ready, 1)

            def one_hots(t):
                s = t.slot
                t.wait(dve, scat_mm, 2, -2)
                for j in range(2):
                    col = t.count(2, j)
                    dve.tensor_scalar(oh_src[s][:, j], iota_s[:], srccol[:, bass.ds(col, 1)], None,
                                      ALU.is_equal).then_inc(hots_ready, 1)
                    dve.tensor_scalar(oh_srcb[s][:, j], iota_s[:], srccol[:, bass.ds(col, 1)], None,
                                      ALU.is_equal).then_inc(hots_ready, 1)
                    dve.tensor_scalar(oh_dst[s][:, j], iota_d[:], dstcol[:, bass.ds(col, 1)], None,
                                      ALU.is_equal).then_inc(hots_ready, 1)

            def flush(t):
                b = dve.value_load(bucket_row[0:1, bass.ds(t.count(1), 1)], min_val=0, max_val=C - 1)
                agg = acc_agg[:, bass.ds(b * F, F)]
                adj = acc_adj[:, bass.ds(b * NP, NP)]
                dve.wait_ge(scat_mm, t.count(2, 1))
                t.wait(dve, flushed, 2, -1)
                dve.tensor_tensor(agg, ps[0:NC, 5], agg, op=ALU.add).then_inc(flushed, 1)
                dve.wait_ge(scat_mm, t.count(2, 2))
                t.wait(dve, flushed, 2)
                dve.tensor_tensor(adj, ps[0:NC, 6:8].rearrange("p b n -> p (b n)")[:, 0:NP], adj,
                                  op=ALU.add).then_inc(flushed, 1)

            rows_lo(Step(None, 0))
            rows_lo(Step(None, 1))

            def edge_step(t):
                one_hots(t)
                edge_feature(t, 0)
                message(t, 0)
                if t.reg is not None or t.c + 2 < STEPS:
                    rows_lo(t.at(2))
                message_lo(t, 0)
                edge_feature(t, 1)
                message(t, 1)
                if t.reg is not None or t.c > 0:
                    flush(t.at(-1))
                message_lo(t, 1)

            steps(dve, STEPS, edge_step)
            flush(Step(None, STEPS - 1))

            def halves(i):
                w = HALF[i % 2]
                return slice((i % 2) * HALF[0], (i % 2) * HALF[0] + w), w

            def turned_lo(name):
                for c in range(C):
                    n = slice(c * NC, c * NC + NC)
                    dve.wait_ge(act_done, ACTS[name] + c + 1)
                    dve.tensor_tensor(ht_lo[:, :, n],
                                      bank(UNIT[name] + c)[:, 0:K * NC].rearrange("p (k n) -> p k n", k=K),
                                      ht_hi[:, :, n], op=ALU.subtract).then_inc(freed, 1)

            turned_lo("aggT")
            for i in range(2 * K):
                cols, w = halves(i)
                dve.wait_ge(act_done, ACTS["mlp1"] + 2 * i + 2)
                dve.tensor_tensor(s1_lo[:, i // 2, cols], z32[:, i % 2, 0:w], s1_hi[:, i // 2, cols],
                                  op=ALU.subtract).then_inc(freed, 1)
            for c in range(C):
                dve.wait_ge(filled, UNIT["mlp2"] + c + 1)
                dve.tensor_tensor(x_res[:, c], bank(UNIT["mlp2"] + c)[0:NC], x_res[:, c], op=ALU.add).then_inc(freed, 1)
            norm(1, freed, UNIT["mlp2"] + C)
            for i in range(2 * C):
                cols = slice(0, 4 * NC) if i % 2 == 0 else slice(4 * NC, N)
                w = 4 * NC if i % 2 == 0 else NC
                dve.wait_ge(act_done, ACTS["adjT"] + 1 + i + 1)
                dve.tensor_tensor(adj_lo[1][:, i // 2, cols], bank(UNIT["adjT"] + i)[0:NC, 0:w],
                                  adj_hi[1][:, i // 2, cols], op=ALU.subtract).then_inc(freed, 1)
            turned_lo("h1T")

            def rows_relu_lo(count, bank_of, acts):
                for c in range(C):
                    dve.wait_ge(act_done, acts(c + 1))
                    dve.scalar_tensor_tensor(out=h_lo[:, c], in0=bank_of(c)[0:NC], scalar=0.0, in1=h_hi[:, c],
                                             op0=ALU.max, op1=ALU.subtract).then_inc(freed, 1)

            def turned_pairs(bank_of, fill, acts):
                for c in range(C):
                    dve.wait_ge(filled, fill(2 * c + 2))
                    dve.wait_ge(act_done, acts(c + 1))
                    dve.tensor_copy(ht_lo[:, :, c * NC:c * NC + NC],
                                    bank_of(2 * c + 1)[:, 0:K * NC].rearrange("p (k n) -> p k n", k=K)).then_inc(freed, 2)

            rows_relu_lo(None, lambda c: bank(UNIT["init"] + c), lambda n: ACTS["init"] + n)
            turned_pairs(lambda n: bank(UNIT["initT"] + n), lambda n: UNIT["initT"] + n,
                         lambda n: ACTS["initT"] + n)

            for d in range(2):
                for i in range(2):
                    cols, w = halves(i)
                    dve.wait_ge(filled, UNIT["degrow"] + 2 * d + i + 1)
                    dve.tensor_scalar(z32[:, i, 0:w], bank(UNIT["degrow"] + 2 * d + i)[:, 0:w], 1.0, None,
                                      ALU.max).then_inc(freed, 1)
                for i in range(2):
                    cols, w = halves(i)
                    dve.wait_ge(freed, UNIT["degrow"] + 2 * d + i + 1)
                    dve.reciprocal(rdeg[d][:, cols], z32[:, i, 0:w]).then_inc(rdeg_ready, 1)
                dve.wait_ge(rdeg_ready, 2 * d + 2)
            dve.wait_ge(pads_ready, 4)
            dve.tensor_reduce(part_col[:, 0], acc3, axis=AX, op=ALU.add).then_inc(deg_step, 1)
            dve.tensor_reduce(part_col[:, 1], adj_hi[1][:], axis=AX, op=ALU.add).then_inc(deg_step, 1)
            dve.tensor_reduce(part_col[:, 2], adj_lo[1][:], axis=AX, op=ALU.add).then_inc(deg_step, 1)
            dve.wait_ge(deg_step, 3)
            dve.tensor_scalar(deg_col[:, 0], part_col[:, 0], 1.0, None, ALU.add).then_inc(deg_step, 1)
            dve.scalar_tensor_tensor(out=deg_col[:, 1], in0=part_col[:, 1], scalar=1.0, in1=part_col[:, 2],
                                     op0=ALU.add, op1=ALU.add).then_inc(deg_step, 1)

            def layer(l, last):
                def count(n):
                    return l * LAYER_UNITS + (UNIT["layer0"] + n)

                def acts(n):
                    return l * LAYER_ACTS + (ACTS["layer0"] + n)

                def scale(i):
                    d = i // 8
                    cols, w = halves(i)
                    dve.wait_ge(filled, count(i + 1))
                    if i < 2:
                        dve.wait_ge(freed, count(0))
                    else:
                        dve.wait_ge(z_lo_ready, l * 16 + i - 1)
                    dve.tensor_tensor(z32[:, i % 2, 0:w], ps[:, i % 8, 0:w], rdeg[d][:, cols], op=ALU.mult).then_inc(freed, 1)

                def low(i):
                    cols, w = halves(i)
                    d, f = i // 8, i % 8 // 2
                    dve.wait_ge(act_done, acts(i + 1))
                    dve.tensor_tensor(z_lo[d][:, f, cols], z32[:, i % 2, 0:w], z_hi[d][:, f, cols],
                                      op=ALU.subtract).then_inc(z_lo_ready, 1)

                scale(0)
                for i in range(1, 16):
                    scale(i)
                    low(i - 1)
                low(15)
                if last:
                    for c in range(C):
                        dve.wait_ge(filled, count(17 + c))
                        dve.scalar_tensor_tensor(out=x_res[:, c], in0=ps[0:NC, (16 + c) % 8], scalar=0.0,
                                                 in1=x_res[:, c], op0=ALU.max, op1=ALU.add).then_inc(freed, 1)
                    return
                rows_relu_lo(None, lambda c: ps[:, (16 + c) % 8], lambda n: acts(16 + n))
                turned_pairs(lambda n: ps[:, (21 + n) % 8], lambda n: count(21 + n), lambda n: acts(21 + n))

            with dve.Fori(0, LAYERS - 1) as l:
                layer(l, False)
            layer(LAYERS - 1, True)

            dve.wait_ge(deg_root, 1)
            dve.reciprocal(dinv_col[:], root_col[:]).then_inc(deg_step, 1)
            norm(2, freed, UNIT["h2T"])
            turned_lo("h2T")
            dve.wait_ge(bias2_in, 16)
            for c in range(C):
                dve.wait_ge(filled, UNIT["lin2"] + c + 1)
                dve.tensor_tensor(g32[:, c], bank(UNIT["lin2"] + c)[0:NC], row_a[0:NC], op=ALU.add).then_inc(freed, 1)
            for c in range(C):
                dve.wait_ge(freed, UNIT["lin2"] + c + 1)
                dve.wait_ge(act_done, ACTS["lin2"] + c + 1)
                dve.scalar_tensor_tensor(out=h_lo[:, c], in0=g32[:, c], scalar=dinv_col[:, 0, c:c + 1],
                                         in1=h_hi[:, c], op0=ALU.mult, op1=ALU.subtract).then_inc(split_g, 1)
            for c in range(C):
                dve.wait_ge(filled, UNIT["conv2"] + c + 1)
                dve.wait_ge(split_g, C)
                dve.tensor_scalar(g32[:, c], bank(UNIT["conv2"] + c)[0:NC], dinv_col[:, 0, c:c + 1], 0.0,
                                  ALU.mult, ALU.max).then_inc(freed, 1)
            for c in range(C):
                dve.wait_ge(freed, UNIT["conv2"] + c + 1)
                dve.tensor_tensor(x_res[:, c], x_res[:, c], g32[:, c], op=ALU.add).then_inc(scaled_x, 1)
            for i in range(2):
                cols, w = halves(i)
                dve.wait_ge(filled, UNIT["sumrow"] + i + 1)
                dve.tensor_scalar(deg_row[:, cols], bank(UNIT["sumrow"] + i)[:, 0:w], 1.0, None, ALU.max).then_inc(freed, 1)
            norm(3, scaled_x, C)
            dve.wait_ge(act_done, ACTS["sumrow"] + 2)
            dve.reciprocal(dinv_row[:], root_row[:]).then_inc(rdeg_ready, 1)
            dve.wait_ge(rdeg_ready, 5)
            dve.wait_ge(bias4_in, 16)
            dve.wait_ge(ln_act, 4 * (1 + C))
            for c in range(C):
                dve.tensor_tensor(x_res[:, c], x_res[:, c], row_b[0:NC], op=ALU.add).then_inc(scaled_x, 1)
            turned_lo("h3T")

            def conv(lin, name, f0, chunks):
                for c in range(C):
                    w = chunks * P
                    dve.wait_ge(act_done, ACTS[lin] + c + 1)
                    dve.scalar_tensor_tensor(out=h_lo[:, c, 0:w], in0=bank(UNIT[lin] + c)[0:NC, 0:w],
                                             scalar=dinv_col[:, 1, c:c + 1], in1=h_hi[:, c, 0:w],
                                             op0=ALU.mult, op1=ALU.subtract).then_inc(freed, 1)
                for i in range(2 * chunks):
                    cols, w = halves(i)
                    f = f0 + i // 2
                    dve.wait_ge(filled, UNIT[name] + i + 1)
                    if i >= 2:
                        dve.wait_ge(act_done, ACTS[name] + 2 * i - 3)
                    dve.tensor_tensor(z32[:, i % 2, 0:w], bank(UNIT[name] + i)[:, 0:w], dinv_row[:, cols],
                                      op=ALU.mult).then_inc(scaled, 1)
                    dve.wait_ge(act_done, ACTS[name] + 2 * i + 2)
                    dve.tensor_tensor(ht_lo[:, f, cols], relu32[:, i % 2, 0:w], ht_hi[:, f, cols],
                                      op=ALU.subtract).then_inc(freed, 1)

            conv("lin_a", "conv_a", 0, 2)
            conv("lin_b", "conv_b", 2, 1)
            conv("lin_c", "conv_c", 3, 1)
            dve.wait_ge(scaled_x, 2 * C)
            for c in range(C):
                dve.wait_ge(filled, UNIT["last"] + c + 1)
                dve.tensor_tensor(x_res[:, c], bank(UNIT["last"] + c)[0:NC], x_res[:, c], op=ALU.add).then_inc(freed, 1)


def kernel(**inputs):
    import numpy as np
    import concourse.bacc as bacc
    from concourse.bass_utils import run_bass_kernel_spmd

    def packed(w):
        return w.reshape(-1, P, w.shape[1]).transpose(1, 0, 2).reshape(P, -1)

    g = {name: np.asarray(v) for name, v in inputs.items()}
    w_self = g["L1_gnn_W_self"]
    fold_a, fold_b, selfw = [], [], []
    for l in range(LAYERS):
        t = w_self[l].T
        selfw.append(packed(t[0:F]))
        fold_a += [packed(g["L1_gnn_W_fwd"][l]), packed(g["L1_gnn_W_bwd"][l])]
        fold_b += [packed(t[F:2 * F]), packed(t[2 * F:3 * F])]
    conv_w = np.concatenate([packed(g["L3_gnn_W1"]), packed(g["L3_gnn_W2"]), packed(g["L3_gnn_W3"])], axis=1)
    conv_w = np.concatenate([conv_w, np.zeros((P, K * F - conv_w.shape[1]), conv_w.dtype)], axis=1)
    conv_bias = np.concatenate([g["L3_gnn_b1"], g["L3_gnn_b2"], g["L3_gnn_b3"]]).reshape(4, P).T
    data = {
        "x": g["x"], "src": g["src"].reshape(EP, ET), "dst": g["dst"].reshape(EP, ET),
        "edge": g["edge_attr_128"],
        "we1": g["L0_gnn_We1"], "be1": g["L0_gnn_be1"].reshape(K, P).T,
        "we2": packed(g["L0_gnn_We2"]), "be2": g["L0_gnn_be2"].reshape(1, F),
        "nodew": np.stack([packed(g["L0_gnn_Wn1"]), packed(g["L0_gnn_Wn2"]), packed(g["L1_gnn_W_init"].T)]),
        "bn1": g["L0_gnn_bn1"].reshape(K, P).T, "bn2": g["L0_gnn_bn2"].reshape(1, F),
        "fold_a": np.stack(fold_a), "fold_b": np.stack(fold_b), "selfw": np.stack(selfw),
        "lin2": packed(g["L2_gnn_W"].T), "b2": g["L2_gnn_b"].reshape(1, F),
        "conv_w": conv_w, "conv_bias": conv_bias,
        "lastw": packed(g["L3_gnn_W4"].T), "b4": g["L3_gnn_b4"].reshape(1, F),
    }
    nc = bacc.Bacc("TRN2", target_bir_lowering=False, num_devices=1)
    arrays, args = {}, {}
    for name, v in data.items():
        v = np.ascontiguousarray(v)
        arrays[f"in_{name}"] = v
        args[name] = nc.dram_tensor(f"in_{name}", v.shape, mybir.dt.from_np(v.dtype), kind="ExternalInput").ap()
    out = nc.dram_tensor("out_0", (N, F), F32, kind="ExternalOutput").ap()
    build(nc, args, out)
    r = run_bass_kernel_spmd(nc, [arrays], core_ids=[0])
    return r.results[0]["out_0"]
```

```python
from contextlib import ExitStack

import concourse.bass as bass
from concourse import mybir

F32 = mybir.dt.float32
F32R = mybir.dt.float32r
BF16 = mybir.dt.bfloat16
F16 = mybir.dt.float16
I32 = mybir.dt.int32
ALU = mybir.AluOpType
ACT = mybir.ActivationFunctionType
AX = mybir.AxisListType.X

P = 128
N = 625
C = 5
NC = N // C
NP = N + 1
HALF = (314, 312)
F = 512
K = F // P
E = 20625
R = 128
EP = 125
ET = E // EP
PAIR = 2 * P
STEPS = (E + C * (PAIR - 1)) // PAIR
TILES = 2 * STEPS
FOLDS = 6
PERM_FOLD = 9
PERM = PERM_FOLD * FOLDS
PERM_RING = 3
LIMB_BITS = P.bit_length() - 1
LIMB_SHIFT, LIMB_MASK = 4, 15
LAYERS = 3
W1C, W2C, W3C = 256, 128, 128

UNITS = [("aggT", 5, 5), ("mlp1", 8, 16), ("adjT", 10, 11), ("mlp2", 5, 0), ("h1T", 5, 5), ("init", 15, 10),
         ("large", 1, 0), ("degrow", 4, 0), ("layer0", 31, 26), ("layer1", 31, 26), ("layer2", 21, 16),
         ("h2T", 5, 5), ("lin2", 5, 5), ("conv2", 5, 0), ("sumrow", 2, 2), ("h3T", 5, 5), ("lin_a", 5, 5),
         ("conv_a", 4, 8), ("lin_b", 5, 5), ("conv_b", 2, 4), ("lin_c", 5, 5), ("conv_c", 2, 4), ("last", 5, 0)]
PERM_UNIT = [PERM_FOLD * u // K for u in range(K + 1)]
WOVEN, OUT_AT, TURN_AT = [], [0] * C, [0] * C
_at = 0
for _c in range(C + 1):
    if _c < C:
        WOVEN.append(("out", _c, _at))
        OUT_AT[_c] = _at
        _at += 1
    if _c > 0:
        WOVEN.append(("turn", _c - 1, _at))
        TURN_AT[_c - 1] = _at
        _at += 2
OUT_END, WOVEN_UNITS = OUT_AT[C - 1] + 1, _at
UNIT, ACTS = {}, {}
_u = _a = 0
for _name, _units, _acts in UNITS:
    UNIT[_name], ACTS[_name] = _u, _a
    _u, _a = _u + _units, _a + _acts
LAYER_UNITS, LAYER_ACTS = 31, 26
WEIGHT_TIMES = (0, 8)
NC_BYTES = C * F * 4
EPS = 1e-5


def each(eng, n, body):
    body(0)
    with eng.Fori(1, n) as m:
        body(m)


def wait_rounds(eng, sem, m, per, add=0):
    if not isinstance(m, int) or m * per + add > 0:
        eng.wait_ge(sem, m * per + add)


class Step:

    def __init__(self, reg, c):
        self.reg, self.c = reg, c

    def at(self, k):
        return Step(self.reg, self.c + k)

    @property
    def slot(self):
        return self.c % 2

    def count(self, per, add=0):
        if self.reg is None:
            return per * self.c + add
        return self.reg * (2 * per) + (per * self.c + add)

    def rounds(self, per):
        if self.reg is None:
            return per * (self.c // 2 + 1)
        return self.reg * per + per * (self.c // 2 + 1)

    def wait(self, eng, sem, per, add=0):
        if self.reg is not None or per * self.c + add > 0:
            eng.wait_ge(sem, self.count(per, add))


def steps(eng, n, body):
    pairs = (n - 5) // 2
    body(Step(None, 0))
    body(Step(None, 1))
    with eng.Fori(0, pairs) as i:
        body(Step(i, 2))
        body(Step(i, 3))
    for c in range(2 + 2 * pairs, n):
        body(Step(None, c))



def build(nc, a, out):
    with ExitStack() as ctx:
        def sem(name):
            return ctx.enter_context(nc.semaphore(name))

        base = (nc.sbuf_base + 63) // 64 * 64
        end = nc.sbuf_usable_end
        ctx.enter_context(nc.sbuf_tensor("arena", [P, end - base - 64], mybir.dt.uint8))
        size = {F32: 4, F32R: 4, I32: 4, BF16: 2, F16: 2}

        class Region:
            def __init__(self, at):
                self.at = at

            def __call__(self, name, shape, dt):
                n = size[dt]
                for s in shape[1:]:
                    n *= s
                t = nc.alloc_sbuf_tensor_at(name, shape, dt, offset=self.at)
                self.at += (n + 31) // 32 * 32
                assert self.at <= end, (name, self.at, end)
                return t

        keep = Region(base)
        x_res = keep("x_res", [NC, C, F], F32)
        part_col = keep("part_col", [NC, 3, C], F32)
        peaks = keep("peaks", [NC, C], F32)
        peak = keep("peak", [NC, 1], F32)
        large = keep("large", [NC, 2], F32R)
        large_any = keep("large_any", [1, 1], I32)
        deg_col = keep("deg_col", [NC, 2, C], F32)
        root_col = keep("root_col", [NC, 2, C], F32)
        dinv_col = keep("dinv_col", [NC, 2, C], F32)
        ident = keep("ident", [P, P], F32)
        ones = keep("ones", [P, P], F32R)
        eps_col = keep("eps_col", [P, 1], F32)
        stats = keep("stats", [NC, C, 6], F32)
        mv = keep("mv", [NC, C, 2], F32)
        std = keep("std", [NC, C], F32)
        rstd = keep("rstd", [NC, C], F32)
        shift = keep("shift", [NC, C], F32)
        be1 = keep("be1", [P, K], F32)
        bn1 = keep("bn1", [P, K], F32)
        conv_bias = keep("conv_bias", [P, 4], F32)
        row_a = keep("row_a", [P, F], F32)
        row_b = keep("row_b", [P, F], F32)
        w_hi = [keep(f"w_hi{i}", [P, K, F], F32R) for i in range(3)]
        w_raw = [Region(keep.at + i * K * F * 4)(f"w_raw{i}", [P, K, F], F32) for i in range(3)]
        w_lo = [keep(f"w_lo{i}", [P, K, F], F32R) for i in range(3)]

        edge = Region(keep.at)
        acc_agg = edge("acc_agg", [NC, C * F], F32)
        acc_adj = edge("acc_adj", [NC, C * NP], F32)
        h32 = edge("h32", [NC, C, F], F32)
        h32_at = edge.at - NC_BYTES
        main = Region(edge.at)
        we1_hi = main("we1_hi", [P, F], F32R)
        we1_raw = Region(main.at)("we1_raw", [P, F], F32)
        we1_lo = main("we1_lo", [P, F], F32R)
        we2_hi = main("we2_hi", [P, K, F], F32R)
        we2_raw = Region(main.at)("we2_raw", [P, K, F], F32)
        we2_lo = main("we2_lo", [P, K, F], F32R)
        table = main("table", [P, TILES, 4], I32)
        bucket_row = main("bucket_row", [1, STEPS], I32)
        srccol = main("srccol", [P, TILES], F32)
        dstcol = main("dstcol", [P, TILES], F32)
        iota_s = main("iota_s", [P, NC + 1], F32)
        iota_d = main("iota_d", [P, NP], F16)
        loop = Region(main.at)
        edge_picks = [loop(f"edge_picks{i}", [P, 2], I32) for i in range(2)]
        node_picks = [loop(f"node_picks{i}", [P, 2], I32) for i in range(2)]
        rbf = [loop(f"rbf{i}", [P, 2, R], F32) for i in range(2)]
        xg = [loop(f"xg{i}", [P, 2, F], F32) for i in range(2)]
        rT_hi = [loop(f"rT_hi{i}", [P, PAIR], F32R) for i in range(2)]
        rT_lo = [loop(f"rT_lo{i}", [P, PAIR], F32R) for i in range(2)]
        s32 = loop("s32", [P, K, PAIR], F32)
        s_hi = [loop(f"s_hi{i}", [P, K, PAIR], F32R) for i in range(2)]
        s_lo = [loop(f"s_lo{i}", [P, K, PAIR], F32R) for i in range(2)]
        feat = [loop(f"feat{j}", [P, F], F32) for j in range(2)]
        msg = [loop(f"msg{j}", [P, F], F32) for j in range(2)]
        m_hi = [loop(f"m_hi{i}", [P, 2, F], F32R) for i in range(2)]
        m_lo = [loop(f"m_lo{i}", [P, 2, F], F32R) for i in range(2)]
        oh_src = [loop(f"oh_src{i}", [P, 2, NC + 1], F32R) for i in range(2)]
        oh_srcb = [loop(f"oh_srcb{i}", [P, 2, NC + 1], BF16) for i in range(2)]
        oh_dst = [loop(f"oh_dst{i}", [P, 2, NP], BF16) for i in range(2)]

        pre = Region(main.at)
        stage = pre("stage", [P, 2, K, F], F32)
        fold_hi = pre("fold_hi", [P, 2, K, F], F32R)
        fold_lo = pre("fold_lo", [P, 2, K, F], F32R)
        empty = Region(pre.at)("empty", [P, TILES * 4], I32)
        folded = pre("folded", [P, K, F], F32)
        src_i = pre("src_i", [EP, ET], I32)
        dst_i = pre("dst_i", [EP, ET], I32)
        src_f = pre("src_f", [EP, ET], F32)
        reach = pre("reach", [EP, C + 1, ET], F32)
        sorted_late = Region(pre.at)
        perm_i = sorted_late("perm_i", [P, 3, TILES], I32)
        perm_e = sorted_late("perm_e", [P, TILES], F32)
        member = pre("member", [EP, C, ET], F32)
        assert sorted_late.at <= pre.at
        rank = pre("rank", [EP, C, ET], F32)
        zeros = pre("zeros", [EP, ET], F32)
        bucket = pre("bucket", [EP, ET], F32)
        pos_f = pre("pos_f", [EP, ET], F32)
        pos_i = pre("pos_i", [EP, ET], I32)
        pos_lo = pre("pos_lo", [EP, ET], I32)
        pos_hi = pre("pos_hi", [EP, ET], I32)
        row_i = pre("row_i", [EP, ET], I32)
        fields = pre("fields", [EP, ET, 4], I32)
        limb_i = pre("limb_i", [EP, 2, PERM], I32)
        limb = pre("limb", [EP, 3, PERM], F32)
        slot_lo = pre("slot_lo", [EP, PERM], F32)
        slot_hi = pre("slot_hi", [EP, PERM], F32)
        hot_lo = [pre(f"hot_lo{i}", [EP, P], F16) for i in range(PERM_RING)]
        hot_hi = [pre(f"hot_hi{i}", [EP, TILES], F16) for i in range(PERM_RING)]
        marked = [pre(f"marked{i}", [EP, 3, TILES], F16) for i in range(PERM_RING)]
        before = pre("before", [P, P], F32)
        ones32 = pre("ones32", [P, P], F32)
        counts32 = pre("counts32", [EP, C], F32)
        total_i = pre("total_i", [EP, C], I32)
        chunks_i = pre("chunks_i", [EP, C], I32)
        chunks_f = pre("chunks_f", [EP, C], F32)
        upto = pre("upto", [EP, C], F32)
        first = pre("first", [EP, C], F32)
        offset = pre("offset", [EP, C], F32)
        step_row = pre("step_row", [1, STEPS], F32)
        bucket_f = [pre(f"bucket_f{i}", [1, STEPS], F32) for i in range(2)]

        node = Region(keep.at)
        z_hi = [None, None]
        z_lo = [None, None]
        z_hi[0] = node("zf_hi", [P, K, NP], F32R)
        z_lo[0] = node("zf_lo", [P, K, NP], F32R)
        z_hi[1] = node("zb_hi", [P, K, NP], F32R)
        z_lo[1] = node("zb_lo", [P, K, NP], F32R)
        adj_hi = [None, None]
        adj_lo = [None, None]
        adj_hi[0] = node("adj_hi", [NC, C, NP], F32R)
        adj_lo[0] = node("adj_lo", [NC, C, NP], F32R)
        adj_hi[1] = node("adjT_hi", [NC, C, NP], F32R)
        adj_lo[1] = node("adjT_lo", [NC, C, NP], F32R)
        share = Region(node.at)
        s1_hi = share("s1_hi", [P, K, NP], F32R)
        s1_lo = share("s1_lo", [P, K, NP], F32R)
        h_hi = node("h_hi", [NC, C, F], F32R)
        h_lo = node("h_lo", [NC, C, F], F32R)
        ht_hi = node("ht_hi", [P, K, NP], F32R)
        ht_lo = node("ht_lo", [P, K, NP], F32R)
        z32 = node("z32", [P, 2, HALF[0]], F32)
        rdeg = [node("rdeg_in", [P, NP], F32), node("rdeg_out", [P, NP], F32)]
        diag = Region(node.at)("diag", [NC, 2, C, NC], F32)
        wstage = node("wstage", [P, K * F], F32)
        late = Region(keep.at)
        relu32 = late("relu32", [P, 2, HALF[0]], F32)
        g32 = late("g32", [NC, C, F], F32)
        deg_row = late("deg_row", [P, NP], F32)
        root_row = late("root_row", [P, NP], F32)
        dinv_row = late("dinv_row", [P, NP], F32)
        assert late.at <= h32_at
        acc3 = acc_adj[:, :].rearrange("p (c n) -> p c n", c=C)
        agg3 = acc_agg[:, :].rearrange("p (c n) -> p c n", c=C)

        ps = ctx.enter_context(nc.psum_tensor("ps", [P, 8, 512], F32))

        h_dram = nc.dram_tensor("h_dram", [N, F], F32, kind="Internal").ap()
        slots_dram = nc.dram_tensor("slots_dram", [P * TILES, 4], I32, kind="Internal").ap()
        fold_dram = nc.dram_tensor("fold_dram", [FOLDS, P, K * F], F32, kind="Internal").ap()

        x_in, edges_in, small_in, h_saved = sem("x_in"), sem("edges_in"), sem("small_in"), sem("h_saved")
        consts_ready = sem("consts_ready")
        ln_stats, ln_act, ln_coef = sem("ln_stats"), sem("ln_act"), sem("ln_coef")
        res_ready = sem("res_ready")
        edge_weights_in, node_weights_in = sem("edge_weights_in"), sem("node_weights_in")
        weights_hi, weights_lo = sem("weights_hi"), sem("weights_lo")
        stage_in, split_hi, split_lo = sem("stage_in"), sem("split_hi"), sem("split_lo")
        fold_mm, fold_ev, fold_st = sem("fold_mm"), sem("fold_ev"), sem("fold_st")
        sort_step, rank_mm = sem("sort_step"), sem("rank_mm")
        empty_saved, ring_filled, table_in, cols_ready = (
            sem("empty_saved"), sem("ring_filled"), sem("table_in"), sem("cols_ready"))
        limbs_ready, hots_made, marks_made, perm_mm = (
            sem("limbs_ready"), sem("hots_made"), sem("marks_made"), sem("perm_mm"))
        perm_out, table_ready = sem("perm_out"), sem("table_ready")
        scattered = [sem(f"scattered{j}") for j in range(5)]
        picked = sem("picked")
        rbf_in = [sem(f"rbf_in{i}") for i in range(2)]
        xg_in = [sem(f"xg_in{i}") for i in range(2)]
        rT_mm, rT_hi_ready, rT_lo_ready = sem("rT_mm"), sem("rT_hi_ready"), sem("rT_lo_ready")
        z1_mm, silu_ready, s_hi_ready, s_lo_ready = sem("z1_mm"), sem("silu_ready"), sem("s_hi_ready"), sem("s_lo_ready")
        feat_mm, feat_ready, msg_ready = sem("feat_mm"), sem("feat_ready"), sem("msg_ready")
        m_hi_ready, m_lo_ready = sem("m_hi_ready"), sem("m_lo_ready")
        hots_ready, scat_mm, flushed = sem("hots_ready"), sem("scat_mm"), sem("flushed")
        filled, freed, act_done = sem("filled"), sem("freed"), sem("act_done")
        wstage_in, w_split, pads_ready = sem("wstage_in"), sem("w_split"), sem("pads_ready")
        adj_split, adj_self = sem("adj_split"), sem("adj_self")
        peak_step = sem("peak_step")
        deg_step, deg_root, scaled = sem("deg_step"), sem("deg_root"), sem("scaled")
        rdeg_ready, scaled_x, rows_part = sem("rdeg_ready"), sem("scaled_x"), sem("rows_part")
        counts_ready, ranks_read = sem("counts_ready"), sem("ranks_read")
        z_lo_ready, split_g = sem("z_lo_ready"), sem("split_g")
        bias2_in, bias4_in, out_saved = sem("bias2_in"), sem("bias4_in"), sem("out_saved")

        WEIGHTS = ((we2_hi, we2_lo, we2_raw), (we1_hi, we1_lo, we1_raw),
                   *((w_hi[i], w_lo[i], w_raw[i]) for i in range(3)))

        block = ctx.enter_context(nc.Block())

        @block.sync
        def _(sp):
            sp.dma_start(src_i[:], a["src"]).then_inc(edges_in, 16)
            sp.dma_start(dst_i[:], a["dst"]).then_inc(edges_in, 16)
            sp.wait_ge(consts_ready, 1)
            sp.dma_start(slots_dram.rearrange("(p t) w -> p (t w)", p=P), empty[:]).then_inc(empty_saved, 16)
            sp.dma_start(stage[:, 0].rearrange("p k f -> p (k f)"), a["fold_a"][0]).then_inc(stage_in, 16)
            sp.dma_start(stage[:, 1].rearrange("p k f -> p (k f)"), a["fold_b"][0]).then_inc(stage_in, 16)
            sp.dma_start(x_res[:], a["x"].rearrange("(c p) f -> p c f", p=NC)).then_inc(x_in, 16)
            sp.dma_start(we2_raw[:].rearrange("p k f -> p (k f)"), a["we2"]).then_inc(edge_weights_in, 16)
            sp.dma_start(we1_raw[:], a["we1"]).then_inc(edge_weights_in, 16)
            for i in range(3):
                sp.dma_start(w_raw[i][:].rearrange("p k f -> p (k f)"), a["nodew"][i]).then_inc(node_weights_in, 16)
            sp.dma_start(be1[:], a["be1"]).then_inc(small_in, 16)
            sp.dma_start(bn1[:], a["bn1"]).then_inc(small_in, 16)
            sp.dma_start(conv_bias[:], a["conv_bias"]).then_inc(small_in, 16)
            sp.dma_start(row_a[:], a["be2"].to_broadcast([P, F])).then_inc(small_in, 16)
            sp.dma_start(row_b[:], a["bn2"].to_broadcast([P, F])).then_inc(small_in, 16)
            sp.wait_ge(ln_act, 1 + C)
            sp.dma_start(h_dram.rearrange("(c p) f -> p c f", p=NC), h32[:]).then_inc(h_saved, 16)

            def load_factors(m):
                sp.wait_ge(split_lo, m * K)
                for part, w in enumerate((a["fold_a"], a["fold_b"])):
                    sp.dma_start(stage[:, part], w[bass.ds(m, 1)].rearrange("m p (k f) -> p (m k) f", k=K)).then_inc(stage_in, 16)

            def save_product(m):
                sp.wait_ge(fold_ev, (m + 1) * K)
                sp.dma_start(fold_dram[bass.ds(m, 1)].rearrange("m p f -> p (m f)"),
                             folded[:].rearrange("p k f -> p (k f)")).then_inc(fold_st, 16)

            with sp.Fori(1, FOLDS) as m:
                load_factors(m)
                save_product(m - 1)
            save_product(FOLDS - 1)

            for j in range(5):
                sp.wait_ge(scattered[j], 16 * len([t for t in range(PERM, ET) if t % 5 == j]))
            sp.dma_start(table[:], slots_dram.rearrange("(p t) w -> p t w", p=P)).then_inc(table_in, 16)

            sp.wait_ge(flushed, 2 * STEPS)
            sp.wait_ge(fold_st, 16 * FOLDS)
            sources = []
            for l in range(LAYERS):
                sources += [a["selfw"][l], fold_dram[2 * l], fold_dram[2 * l + 1]]
            sources += [a["lin2"], a["conv_w"], a["lastw"]]
            for j, source in enumerate(sources):
                if j == 0:
                    sp.wait_ge(filled, UNIT["aggT"] + 1)
                    sp.dma_start(row_a[:], a["b2"].to_broadcast([P, F])).then_inc(bias2_in, 16)
                if j:
                    sp.wait_ge(w_split, 2 * j)
                if j == 3 * LAYERS:
                    sp.wait_ge(adj_self, 3 * C + 1)
                sp.dma_start(wstage[:], source).then_inc(wstage_in, 16)
            sp.wait_ge(freed, UNIT["h1T"])
            sp.dma_start(row_b[:], a["b4"].to_broadcast([P, F])).then_inc(bias4_in, 16)
            out3 = out.rearrange("(c p) f -> c p f", p=NC)
            for c in range(C):
                sp.wait_ge(freed, UNIT["last"] + c + 1)
                sp.dma_start(out3[c], x_res[:, c]).then_inc(out_saved, 16)
            sp.wait_ge(out_saved, 16 * C)

        @block.gpsimd
        def _(pool):
            pool.memset(empty[:], 0).then_inc(consts_ready, 1)
            pool.memset(eps_col[:], EPS).then_inc(consts_ready, 1)
            pool.memset(zeros[:], 0.0).then_inc(consts_ready, 1)
            pool.memset(ones[:].bitcast(F32), 1.0).then_inc(consts_ready, 1)
            pool.memset(ones32[:], 1.0).then_inc(consts_ready, 1)
            pool.memset(ident[:], 0.0).then_inc(consts_ready, 1)
            pool.iota(fields[:, :, 0], pattern=[[1, ET]], base=0, channel_multiplier=ET).then_inc(consts_ready, 1)
            pool.iota(step_row[:], pattern=[[1, STEPS]], base=0, channel_multiplier=0,
                      allow_small_or_imprecise_dtypes=True).then_inc(consts_ready, 1)
            pool.iota(iota_s[:], pattern=[[1, NC + 1]], base=1, channel_multiplier=0,
                      allow_small_or_imprecise_dtypes=True).then_inc(consts_ready, 1)
            pool.iota(iota_d[:], pattern=[[1, NP]], base=0, channel_multiplier=0,
                      allow_small_or_imprecise_dtypes=True).then_inc(consts_ready, 1)
            pool.wait_ge(consts_ready, 10)
            pool.affine_select(out=ident[:], in_=ident[:], compare_op=ALU.not_equal, fill=1.0,
                               base=0, pattern=[[-1, P]], channel_multiplier=1).then_inc(consts_ready, 1)
            pool.affine_select(out=before[:], in_=ones32[:], compare_op=ALU.is_gt, fill=0.0,
                               base=0, pattern=[[1, P]], channel_multiplier=-1).then_inc(consts_ready, 1)
            pool.memset(acc_agg[:], 0.0).then_inc(consts_ready, 1)
            pool.memset(acc_adj[:], 0.0).then_inc(consts_ready, 1)

            pool.wait_ge(empty_saved, 16)
            pool.wait_ge(rows_part, 3 * C + 5)
            for t in range(PERM, ET):
                pool.indirect_dma_start(
                    slots_dram, bass.IndirectOffsetOnAxis(ap=row_i[:, t:t + 1], axis=0),
                    fields[:, t], None).then_inc(scattered[t % 5], 16)

            pool.wait_ge(table_ready, 3)
            pool.wait_ge(h_saved, 16)

            def pick_edges(t):
                t.wait(pool, rT_mm, 1, -1)
                pool.tensor_copy(edge_picks[t.slot][:], table[:, bass.ds(t.count(2), 2), 0]).then_inc(picked, 1)

            def pick_nodes(t):
                t.wait(pool, msg_ready, 2, -2)
                pool.tensor_copy(node_picks[t.slot][:], table[:, bass.ds(t.count(2), 2), 2]).then_inc(picked, 1)

            def gather_edges(t):
                for j in range(2):
                    pool.indirect_dma_start(
                        rbf[t.slot][:, j], None, a["edge"],
                        bass.IndirectOffsetOnAxis(ap=edge_picks[t.slot][:, j:j + 1], axis=0)).then_inc(rbf_in[t.slot], 16)

            def gather_nodes(t):
                for j in range(2):
                    pool.indirect_dma_start(
                        xg[t.slot][:, j], None, h_dram,
                        bass.IndirectOffsetOnAxis(ap=node_picks[t.slot][:, j:j + 1], axis=0)).then_inc(xg_in[t.slot], 16)

            def silu_lo(t):
                s = t.slot
                pool.wait_ge(s_hi_ready, t.count(1, 1))
                t.wait(pool, feat_mm, 2, -2)
                pool.tensor_tensor(s_lo[s][:], s32[:], s_hi[s][:], op=ALU.subtract).then_inc(s_lo_ready, 1)

            pool.wait_ge(split_lo, K * FOLDS)
            for c in range(2):
                pick_edges(Step(None, c))
            pick_nodes(Step(None, 0))
            pool.wait_ge(picked, 3)
            gather_edges(Step(None, 0))
            gather_edges(Step(None, 1))
            gather_nodes(Step(None, 0))
            pick_edges(Step(None, 2))
            pool.wait_ge(picked, 4)
            gather_edges(Step(None, 2))
            silu_lo(Step(None, 0))

            def edge_step(t):
                def within(k):
                    return t.reg is not None or t.c + k < STEPS

                if within(3):
                    pick_edges(t.at(3))
                if within(1):
                    pick_nodes(t.at(1))
                    pool.wait_ge(picked, t.count(2, 6) if within(3) else t.c + STEPS + 2)
                    silu_lo(t.at(1))
                if within(1):
                    gather_nodes(t.at(1))
                if within(3):
                    gather_edges(t.at(3))

            steps(pool, STEPS, edge_step)

            pool.wait_ge(flushed, 2 * STEPS)
            for m in (adj_hi[1], adj_lo[1], ht_hi, ht_lo):
                pool.memset(m[:, :, N:NP].bitcast(F32), 0.0).then_inc(pads_ready, 1)
            pool.wait_ge(small_in, 80)
            for c in range(C):
                pool.tensor_tensor(x_res[:, c], x_res[:, c], h32[:, c], op=ALU.add).then_inc(res_ready, 1)
            for c in range(C):
                pool.wait_ge(res_ready, c + 1)
                pool.tensor_tensor(x_res[:, c], x_res[:, c], row_b[0:NC], op=ALU.add).then_inc(res_ready, 1)
            pool.wait_ge(act_done, ACTS["adjT"] + 2 * C + 1)
            pool.tensor_tensor(adj_lo[0][:], acc3, adj_hi[0][:], op=ALU.subtract).then_inc(adj_split, 1)

            def add_loops():
                pool.wait_ge(filled, UNIT["layer2"] + 16)
                for c in range(C):
                    d = slice(c * NC, c * NC + NC)
                    pool.tensor_tensor(diag[:, 0, c], adj_hi[0][:, c, d], adj_lo[0][:, c, d],
                                       op=ALU.add).then_inc(adj_self, 1)
                pool.wait_ge(adj_self, C)
                pool.tensor_tensor(diag[:, 1], diag[:, 0], ident[0:NC, None, 0:NC].to_broadcast([NC, C, NC]),
                                   op=ALU.add).then_inc(adj_self, 1)
                pool.wait_ge(adj_self, C + 1)
                for c in range(C):
                    d = slice(c * NC, c * NC + NC)
                    pool.tensor_copy(adj_hi[0][:, c, d], diag[:, 1, c]).then_inc(adj_self, 1)
                pool.wait_ge(adj_self, 2 * C + 1)
                for c in range(C):
                    d = slice(c * NC, c * NC + NC)
                    pool.tensor_tensor(adj_lo[0][:, c, d], diag[:, 1, c], adj_hi[0][:, c, d],
                                       op=ALU.subtract).then_inc(adj_self, 1)

            for j in range(3 * (LAYERS + 1)):
                if j == 3 * LAYERS:
                    pool.wait_ge(w_split, 2 * j)
                    add_loops()
                if j < 3 * LAYERS and j % 3 == 2:
                    continue
                pool.wait_ge(w_split, 2 * j + 1)
                pool.tensor_tensor(w_lo[j % 3][:].rearrange("p k f -> p (k f)"), wstage[:],
                                   w_hi[j % 3][:].rearrange("p k f -> p (k f)"), op=ALU.subtract).then_inc(w_split, 1)

        @block.scalar
        def _(act):
            act.wait_ge(consts_ready, 11)

            def norm(k):
                act.wait_ge(ln_stats, 2 * C * (k + 1))
                act.activation(std[:], mv[:, :, 1], ACT.Sqrt, bias=eps_col[0:NC, :]).then_inc(ln_act, 1)
                act.wait_ge(ln_coef, 2 * (k + 1))
                for c in range(C):
                    act.activation(h32[:, c], x_res[:, c], ACT.Relu, bias=shift[:, c:c + 1],
                                   scale=rstd[:, c:c + 1]).then_inc(ln_act, 1)

            def weights_high(start, end):
                for i in range(start, end):
                    if i < 2:
                        act.wait_ge(edge_weights_in, 32)
                    else:
                        act.wait_ge(node_weights_in, 48)
                    act.activation(WEIGHTS[i][0][:], WEIGHTS[i][2][:], ACT.Copy).then_inc(weights_hi, 1)

            def fold(m):
                act.wait_ge(stage_in, (m + 1) * 32)
                wait_rounds(act, fold_mm, m, K)
                for k in range(K):
                    act.activation(fold_hi[:, :, k], stage[:, :, k], ACT.Copy).then_inc(split_hi, 1)
                if isinstance(m, int):
                    weights_high(0, 2)
                    norm(0)
                    act.wait_ge(limbs_ready, 1)
                for u in range(K):
                    for i in range(PERM_UNIT[u], PERM_UNIT[u + 1]):
                        act.wait_ge(hots_made, (m * PERM_FOLD + i) * 3 + 2)
                        for part in (1, 2):
                            act.activation(marked[i % PERM_RING][:, part], hot_hi[i % PERM_RING][:], ACT.Copy,
                                           scale=limb[:, part, bass.ds(m * PERM_FOLD + i, 1)]).then_inc(marks_made, 1)
                    if u == 0:
                        wait_rounds(act, fold_st, m, 16)
                    act.wait_ge(fold_mm, m * K + u + 1)
                    act.activation(folded[:, u], ps[:, 1 + u], ACT.Copy).then_inc(fold_ev, 1)

            act.wait_ge(empty_saved, 16)
            each(act, FOLDS, fold)
            weights_high(2, len(WEIGHTS))

            def rows_hi(t):
                s = t.slot
                act.wait_ge(rT_mm, t.count(1, 1))
                t.wait(act, z1_mm, 2, -2)
                act.activation(rT_hi[s][:], ps[:, 0, 0:PAIR], ACT.Copy).then_inc(rT_hi_ready, 1)

            def silu(t):
                s = t.slot
                t.wait(act, s_lo_ready, 1)
                t.wait(act, s_hi_ready, 1)
                for u in range(K):
                    act.wait_ge(z1_mm, t.count(2, u // 2 + 1))
                    act.activation(s32[:, u], ps[:, 1 + u // 2, (u % 2) * PAIR:(u % 2) * PAIR + PAIR],
                                   ACT.Silu, bias=be1[:, u:u + 1]).then_inc(silu_ready, 1)
                act.wait_ge(silu_ready, t.count(K, K))
                t.wait(act, feat_mm, 2, -2)
                act.activation(s_hi[s][:], s32[:], ACT.Copy).then_inc(s_hi_ready, 1)

            def message_hi(t, j):
                s = t.slot
                act.wait_ge(msg_ready, t.count(2, j + 1))
                t.wait(act, scat_mm, 2, -2)
                act.activation(m_hi[s][:, j], msg[j][:], ACT.Copy).then_inc(m_hi_ready, 1)

            act.wait_ge(split_lo, K * FOLDS)
            act.wait_ge(small_in, 80)
            rows_hi(Step(None, 0))
            silu(Step(None, 0))
            rows_hi(Step(None, 1))

            def edge_step(t):
                if t.reg is not None or t.c + 1 < STEPS:
                    silu(t.at(1))
                if t.reg is not None or t.c + 2 < STEPS:
                    rows_hi(t.at(2))
                message_hi(t, 0)
                message_hi(t, 1)

            steps(act, STEPS, edge_step)

            def copy_units(stage_name, n, view, func=ACT.Copy):
                for i in range(n):
                    act.wait_ge(filled, UNIT[stage_name] + i + 1)
                    dst, src = view(i)
                    act.activation(dst, src, func).then_inc(act_done, 1)

            def bank(u):
                return ps[:, u % 8]

            def turned(stage_name):
                return lambda c: (ht_hi[:, :, c * NC:c * NC + NC],
                                  bank(UNIT[stage_name] + c)[:, 0:K * NC].rearrange("p (k n) -> p k n", k=K))

            act.wait_ge(flushed, 2 * STEPS)
            copy_units("aggT", C, turned("aggT"))
            for i in range(2 * K):
                u = UNIT["mlp1"] + i
                g, half, w = i // 2, i % 2, HALF[i % 2]
                cols = slice(half * HALF[0], half * HALF[0] + w)
                act.wait_ge(filled, u + 1)
                if i >= 2:
                    act.wait_ge(freed, u - 1)
                act.activation(z32[:, i % 2, 0:w], bank(u)[:, 0:w], ACT.Silu, bias=bn1[:, g:g + 1]).then_inc(act_done, 1)
                act.wait_ge(act_done, ACTS["mlp1"] + 2 * i + 1)
                act.activation(s1_hi[:, g, cols], z32[:, i % 2, 0:w], ACT.Copy).then_inc(act_done, 1)

            def adjT_hi(i):
                j, part = i // 2, i % 2
                cols = slice(0, 4 * NC) if part == 0 else slice(4 * NC, N)
                w = 4 * NC if part == 0 else NC
                return adj_hi[1][:, j, cols], bank(UNIT["adjT"] + i)[0:NC, 0:w]

            copy_units("adjT", 2 * C, adjT_hi)
            act.activation(adj_hi[0][:], acc3, ACT.Copy).then_inc(act_done, 1)
            norm(1)
            copy_units("h1T", C, turned("h1T"))

            def out_and_turned(count, bank_of):
                for what, c, at in WOVEN:
                    act.wait_ge(filled, count(at + 1))
                    b = bank_of(at)
                    if what == "out":
                        act.activation(h_hi[:, c], b[0:NC], ACT.Relu).then_inc(act_done, 1)
                    else:
                        act.activation(ht_hi[:, :, c * NC:c * NC + NC],
                                       b[:, 0:K * NC].rearrange("p (k n) -> p k n", k=K),
                                       ACT.Copy).then_inc(act_done, 1)

            out_and_turned(lambda n: UNIT["init"] + n, lambda n: bank(UNIT["init"] + n))

            def weight_high(slot, j):
                act.wait_ge(wstage_in, 16 * j + 16)
                act.activation(w_hi[slot][:].rearrange("p k f -> p (k f)"), wstage[:], ACT.Copy).then_inc(w_split, 1)

            def layer(l, last):
                def count(n):
                    return l * LAYER_UNITS + (UNIT["layer0"] + n)

                for i in range(16):
                    if i in WEIGHT_TIMES:
                        slot = WEIGHT_TIMES.index(i)
                        weight_high(slot, l * 3 + slot)
                    d, f, half, w = i // 8, i % 8 // 2, i % 2, HALF[i % 2]
                    cols = slice(half * HALF[0], half * HALF[0] + w)
                    act.wait_ge(freed, count(i + 1))
                    act.activation(z_hi[d][:, f, cols], z32[:, i % 2, 0:w], ACT.Copy).then_inc(act_done, 1)
                weight_high(2, l * 3 + 2)
                if last:
                    return
                out_and_turned(lambda n: count(16 + n), lambda n: ps[:, (16 + n) % 8])

            with act.Fori(0, LAYERS - 1) as l:
                layer(l, False)
            layer(LAYERS - 1, True)

            act.wait_ge(filled, UNIT["layer2"] + 16 + C)
            weight_high(0, 3 * LAYERS)
            act.wait_ge(deg_step, 5)
            act.activation(root_col[:], deg_col[:], ACT.Sqrt).then_inc(deg_root, 1)
            norm(2)
            copy_units("h2T", C, turned("h2T"))
            for c in range(C):
                act.wait_ge(freed, UNIT["lin2"] + c + 1)
                act.activation(h_hi[:, c], g32[:, c], ACT.Copy, scale=dinv_col[:, 0, c:c + 1]).then_inc(act_done, 1)
            weight_high(1, 3 * LAYERS + 1)
            for half in range(2):
                act.wait_ge(freed, UNIT["sumrow"] + half + 1)
                cols = slice(half * HALF[0], half * HALF[0] + HALF[half])
                act.activation(root_row[:, cols], deg_row[:, cols], ACT.Sqrt).then_inc(act_done, 1)
            weight_high(2, 3 * LAYERS + 2)
            norm(3)
            copy_units("h3T", C, turned("h3T"))

            def conv(name, lin, f0, chunks):
                for c in range(C):
                    act.wait_ge(filled, UNIT[lin] + c + 1)
                    w = chunks * P
                    act.activation(h_hi[:, c, 0:w], bank(UNIT[lin] + c)[0:NC, 0:w], ACT.Copy,
                                   scale=dinv_col[:, 1, c:c + 1]).then_inc(act_done, 1)
                for i in range(2 * chunks):
                    u = UNIT[name] + i
                    f, half, w = f0 + i // 2, i % 2, HALF[i % 2]
                    cols = slice(half * HALF[0], half * HALF[0] + w)
                    act.wait_ge(scaled, 2 * (f0 + i // 2) + half + 1)
                    if i >= 2:
                        act.wait_ge(freed, u - 1)
                    act.activation(relu32[:, i % 2, 0:w], z32[:, i % 2, 0:w], ACT.Relu,
                                   bias=conv_bias[:, f:f + 1]).then_inc(act_done, 1)
                    act.wait_ge(act_done, ACTS[name] + 2 * i + 1)
                    act.activation(ht_hi[:, f, cols], relu32[:, i % 2, 0:w], ACT.Copy).then_inc(act_done, 1)

            conv("conv_a", "lin_a", 0, 2)
            conv("conv_b", "lin_b", 2, 1)
            conv("conv_c", "lin_c", 3, 1)

        @block.tensor
        def _(pe):
            def three(outp, left, right, start, stop):
                (lh, ll), (rh, rl) = left, right
                pe.matmul(outp, lh, rh, start=start, stop=False)
                pe.matmul(outp, lh, rl, start=False, stop=False)
                return pe.matmul(outp, ll, rh, start=False, stop=stop)

            def by_exact(outp, left, right, start, stop):
                (lh, ll), (rh, _) = left, right
                pe.matmul(outp, lh, rh, start=start, stop=False)
                return pe.matmul(outp, ll, rh, start=False, stop=stop)

            def exact_by(outp, left, right, start, stop):
                (lh, _), (rh, rl) = left, right
                pe.matmul(outp, lh, rh, start=start, stop=False)
                return pe.matmul(outp, lh, rl, start=False, stop=stop)

            pe.wait_ge(consts_ready, 12)
            pe.wait_ge(counts_ready, 1)
            pe.matmul(ps[0:EP, 0, 0:C], before[0:EP, 0:EP], counts32[:], start=True, stop=True).then_inc(rank_mm, 1)
            pe.matmul(ps[0:EP, 1, 0:C], ones32[0:EP, 0:EP], counts32[:], start=True, stop=True).then_inc(rank_mm, 1)
            pe.wait_ge(ranks_read, 1)

            def fold(m):
                for u in range(K):
                    wait_rounds(pe, fold_ev, m, K, u + 1 - K)
                    for k in range(K):
                        if u == 0:
                            pe.wait_ge(split_hi, m * K + k + 1)
                            pe.wait_ge(split_lo, m * K + k + 1)
                        f = slice(u * P, u * P + P)
                        mm = three(ps[:, 1 + u], (fold_hi[:, 0, k, f], fold_lo[:, 0, k, f]),
                                   (fold_hi[:, 1, k], fold_lo[:, 1, k]), k == 0, k == K - 1)
                    mm.then_inc(fold_mm, 1)
                    for i in range(PERM_UNIT[u], PERM_UNIT[u + 1]):
                        pe.wait_ge(hots_made, (m * PERM_FOLD + i) * 3 + 3)
                        pe.wait_ge(marks_made, (m * PERM_FOLD + i) * 2 + 2)
                        pe.matmul(ps[:, 5, 0:3 * TILES], hot_lo[i % PERM_RING][:],
                                  marked[i % PERM_RING][:].rearrange("p b t -> p (b t)"),
                                  start=isinstance(m, int) and m == 0 and i == 0,
                                  stop=isinstance(m, int) and m == FOLDS - 1 and i == PERM_FOLD - 1).then_inc(perm_mm, 1)

            fold(0)
            with pe.Fori(1, FOLDS - 1) as m:
                fold(m)
            fold(FOLDS - 1)
            pe.wait_ge(fold_ev, K * FOLDS)

            def turn_rows(t):
                s = t.slot
                pe.wait_ge(rbf_in[s], t.rounds(32))
                t.wait(pe, rT_lo_ready, 1)
                pe.transpose(ps[:, 0, 0:P], rbf[s][:, 0], ident[:])
                pe.transpose(ps[:, 0, P:PAIR], rbf[s][:, 1], ident[:]).then_inc(rT_mm, 1)

            def first_layer(t):
                s = t.slot
                pe.wait_ge(rT_hi_ready, t.count(1, 1))
                pe.wait_ge(rT_lo_ready, t.count(1, 1))
                t.wait(pe, silu_ready, K)
                for u in range(K):
                    f = slice(u * P, u * P + P)
                    mm = three(ps[:, 1 + u // 2, (u % 2) * PAIR:(u % 2) * PAIR + PAIR],
                               (we1_hi[:, f], we1_lo[:, f]), (rT_hi[s][:], rT_lo[s][:]), True, True)
                    if u % 2:
                        mm.then_inc(z1_mm, 1)

            def second_layer(t, j):
                s = t.slot
                e = slice(j * P, j * P + P)
                pe.wait_ge(s_hi_ready, t.count(1, 1))
                pe.wait_ge(s_lo_ready, t.count(1, 1))
                t.wait(pe, feat_ready, 2, j - 1)
                for k in range(K):
                    mm = three(ps[:, 3 + j], (s_hi[s][:, k, e], s_lo[s][:, k, e]),
                               (we2_hi[:, k], we2_lo[:, k]), k == 0, k == K - 1)
                mm.then_inc(feat_mm, 1)

            def scatter(t):
                s = t.slot
                pe.wait_ge(m_hi_ready, t.count(2, 2))
                pe.wait_ge(m_lo_ready, t.count(2, 2))
                pe.wait_ge(hots_ready, t.count(6, 6))
                t.wait(pe, flushed, 2, -1)
                for j in range(2):
                    pe.matmul(ps[0:NC, 5], oh_src[s][:, j, 0:NC], m_hi[s][:, j], start=j == 0, stop=False)
                    mm = pe.matmul(ps[0:NC, 5], oh_src[s][:, j, 0:NC], m_lo[s][:, j], start=False, stop=j == 1)
                mm.then_inc(scat_mm, 1)
                t.wait(pe, flushed, 2)
                for j in range(2):
                    pe.matmul(ps[0:NC, 6], oh_srcb[s][:, j, 0:NC], oh_dst[s][:, j, 0:512], start=j == 0, stop=j == 1)
                for j in range(2):
                    mm = pe.matmul(ps[0:NC, 7, 0:NP - 512], oh_srcb[s][:, j, 0:NC], oh_dst[s][:, j, 512:NP],
                                   start=j == 0, stop=j == 1)
                mm.then_inc(scat_mm, 1)

            pe.wait_ge(weights_hi, 2)
            pe.wait_ge(weights_lo, 2)
            turn_rows(Step(None, 0))
            first_layer(Step(None, 0))
            turn_rows(Step(None, 1))

            def edge_step(t):
                if t.reg is not None or t.c + 1 < STEPS:
                    first_layer(t.at(1))
                second_layer(t, 0)
                if t.reg is not None or t.c + 2 < STEPS:
                    turn_rows(t.at(2))
                second_layer(t, 1)
                if t.reg is not None or t.c > 0:
                    scatter(t.at(-1))

            steps(pe, STEPS, edge_step)
            scatter(Step(None, STEPS - 1))

            def unit(u):
                if u >= 8:
                    pe.wait_ge(freed, u - 7)
                return ps[:, u % 8]

            def turn(stage_name, src, ready, *need):
                for c in range(C):
                    pe.wait_ge(ready, need[0] + c if len(need) == 1 else need[0])
                    b = unit(UNIT[stage_name] + c)
                    for k in range(K):
                        mm = pe.transpose(b[:, k * NC:k * NC + NC], src(c, k), ident[0:NC, 0:NC])
                    mm.then_inc(filled, 1)

            def halves(i):
                w = HALF[i % 2]
                return slice((i % 2) * HALF[0], (i % 2) * HALF[0] + w), w

            def ht(k, c):
                n = slice(c * NC, c * NC + NC)
                return ht_hi[:, k, n], ht_lo[:, k, n]

            def linear(stage_name, slot, width, need, at=0, ks=range(K)):
                ks = list(ks)
                hi = w_hi[slot][:].rearrange("p k f -> p (k f)")
                lo = w_lo[slot][:].rearrange("p k f -> p (k f)")
                for c in range(C):
                    pe.wait_ge(act_done, need(c)[0])
                    pe.wait_ge(freed, need(c)[1])
                    b = unit(UNIT[stage_name] + c)
                    for n, k in enumerate(ks):
                        w = slice(at + n * width, at + n * width + width)
                        mm = three(b[0:NC, 0:width], ht(k, c), (hi[:, w], lo[:, w]), n == 0, n == len(ks) - 1)
                    mm.then_inc(filled, 1)

            def after_turn(stage_name):
                return lambda c: (ACTS[stage_name] + c + 1, UNIT[stage_name] + c + 1)

            pe.wait_ge(flushed, 2 * STEPS)
            pe.wait_ge(weights_hi, len(WEIGHTS))
            pe.wait_ge(weights_lo, len(WEIGHTS))
            turn("aggT", lambda c, k: agg3[:, c, k * P:k * P + P], flushed, 2 * STEPS, 0)
            pe.wait_ge(pads_ready, 4)
            pe.wait_ge(act_done, ACTS["aggT"] + C)
            pe.wait_ge(freed, UNIT["aggT"] + C)
            for i in range(2 * K):
                g = slice(i // 2 * P, i // 2 * P + P)
                cols, w = halves(i)
                b = unit(UNIT["mlp1"] + i)
                for k in range(K):
                    mm = three(b[:, 0:w], (w_hi[0][:, k, g], w_lo[0][:, k, g]),
                               (ht_hi[:, k, cols], ht_lo[:, k, cols]), k == 0, k == K - 1)
                mm.then_inc(filled, 1)
            for j in range(C):
                n = slice(j * NC, j * NC + NC)
                for part in range(2):
                    b = unit(UNIT["adjT"] + 2 * j + part)
                    for c in (range(4) if part == 0 else [4]):
                        at = c * NC if part == 0 else 0
                        mm = pe.transpose(b[0:NC, at:at + NC], acc3[:, c, n], ident[0:NC, 0:NC])
                    mm.then_inc(filled, 1)

            for c in range(C):
                last = 2 * K - 1 if c < 2 else 2 * K
                pe.wait_ge(act_done, ACTS["mlp1"] + 2 * last)
                pe.wait_ge(freed, UNIT["mlp1"] + last)
                n = slice(c * NC, c * NC + NC)
                b = unit(UNIT["mlp2"] + c)
                for k in range(K):
                    mm = three(b[0:NC], (s1_hi[:, k, n], s1_lo[:, k, n]), (w_hi[1][:, k], w_lo[1][:, k]),
                               k == 0, k == K - 1)
                mm.then_inc(filled, 1)

            turn("h1T", lambda c, k: h32[:, c, k * P:k * P + P], ln_act, 2 * (1 + C) - C + 1)

            def out_and_turn(count, unit_of, out_chunk):
                for what, c, at in WOVEN:
                    if what == "out":
                        out_chunk(c, unit_of(at)).then_inc(filled, 1)
                        continue
                    pe.wait_ge(freed, count(OUT_AT[c] + 1))
                    for part, src in enumerate((h_hi, h_lo)):
                        b = unit_of(at + part)
                        for k in range(K):
                            mm = pe.transpose(b[:, k * NC:k * NC + NC],
                                              src[:, c, k * P:k * P + P].bitcast(F32), ident[0:NC, 0:NC])
                        mm.then_inc(filled, 1)

            def init_chunk(c, b):
                pe.wait_ge(act_done, ACTS["h1T"] + c + 1)
                pe.wait_ge(freed, UNIT["h1T"] + c + 1)
                for k in range(K):
                    mm = three(b[0:NC], ht(k, c), (w_hi[2][:, k], w_lo[2][:, k]), k == 0, k == K - 1)
                return mm

            out_and_turn(lambda n: UNIT["init"] + n, lambda n: unit(UNIT["init"] + n), init_chunk)

            pe.wait_ge(peak_step, 3)
            pe.matmul(unit(UNIT["large"])[:, 0:2], ones[0:NC, :], large[:], start=True, stop=True).then_inc(filled, 1)

            pe.wait_ge(adj_split, 1)
            for d in range(2):
                for i in range(2):
                    cols, w = halves(i)
                    b = unit(UNIT["degrow"] + 2 * d + i)
                    for c in range(C):
                        pe.matmul(b[:, 0:w], ones[0:NC, :], adj_hi[d][:, c, cols], start=c == 0, stop=False)
                        mm = pe.matmul(b[:, 0:w], ones[0:NC, :], adj_lo[d][:, c, cols], start=False, stop=c == C - 1)
                    mm.then_inc(filled, 1)

            def layer(l, last):
                def count(n):
                    return l * LAYER_UNITS + (UNIT["layer0"] + n)

                def layer_unit(n):
                    pe.wait_ge(freed, count(n - 6 if n < 8 else n - 7))
                    return ps[:, n % 8]

                pe.wait_ge(freed, count(OUT_END - WOVEN_UNITS))
                def sums(product):
                    for i in range(16):
                        d, f = i // 8, i % 8 // 2
                        cols, w = halves(i)
                        b = layer_unit(i)
                        fs = slice(f * P, f * P + P)
                        for c in range(C):
                            mm = product(b[:, 0:w], (h_hi[:, c, fs], h_lo[:, c, fs]),
                                         (adj_hi[d][:, c, cols], adj_lo[d][:, c, cols]), c == 0, c == C - 1)
                        mm.then_inc(filled, 1)

                with pe.If(any_large > 0):
                    sums(three)
                with pe.Else():
                    sums(by_exact)
                def out_chunk(c, b):
                    n = slice(c * NC, c * NC + NC)
                    for m in range(3):
                        if c == 0:
                            pe.wait_ge(w_split, l * 6 + 2 * (m + 1))
                        if c == 0 and m:
                            pe.wait_ge(z_lo_ready, l * 16 + 8 * m)
                        for k in range(K):
                            left = ht(k, c) if m == 0 else (z_hi[m - 1][:, k, n], z_lo[m - 1][:, k, n])
                            mm = three(b[0:NC], left, (w_hi[m][:, k], w_lo[m][:, k]),
                                       m == 0 and k == 0, m == 2 and k == K - 1)
                    return mm

                if last:
                    for c in range(C):
                        out_chunk(c, layer_unit(16 + c)).then_inc(filled, 1)
                else:
                    out_and_turn(lambda n: count(16 + n), lambda n: layer_unit(16 + n), out_chunk)

            pe.wait_ge(freed, UNIT["layer0"])
            any_large = pe.value_load(large_any[0:1, 0:1], min_val=0, max_val=NC)
            with pe.Fori(0, LAYERS - 1) as l:
                layer(l, False)
            layer(LAYERS - 1, True)

            pe.wait_ge(freed, UNIT["h2T"])
            turn("h2T", lambda c, k: h32[:, c, k * P:k * P + P], ln_act, 3 * (1 + C) - C + 1)
            pe.wait_ge(w_split, 2 * 3 * LAYERS + 2)
            linear("lin2", 0, F, after_turn("h2T"))
            pe.wait_ge(adj_self, 3 * C + 1)
            def conv2_sums(product):
                for c in range(C):
                    n = slice(c * NC, c * NC + NC)
                    b = unit(UNIT["conv2"] + c)
                    for q in range(C):
                        if c == 0:
                            pe.wait_ge(act_done, ACTS["lin2"] + q + 1)
                            pe.wait_ge(split_g, q + 1)
                        mm = product(b[0:NC], (adj_hi[0][:, q, n], adj_lo[0][:, q, n]), (h_hi[:, q], h_lo[:, q]),
                                     q == 0, q == C - 1)
                    mm.then_inc(filled, 1)

            with pe.If(any_large > 0):
                conv2_sums(three)
            with pe.Else():
                conv2_sums(exact_by)
            for i in range(2):
                cols, w = halves(i)
                b = unit(UNIT["sumrow"] + i)
                for c in range(C):
                    pe.matmul(b[:, 0:w], ones[0:NC, :], adj_hi[0][:, c, cols], start=c == 0, stop=False)
                    mm = pe.matmul(b[:, 0:w], ones[0:NC, :], adj_lo[0][:, c, cols], start=False, stop=c == C - 1)
                mm.then_inc(filled, 1)

            turn("h3T", lambda c, k: h32[:, c, k * P:k * P + P], ln_act, 4 * (1 + C) - C + 1)
            pe.wait_ge(w_split, 2 * 3 * LAYERS + 4)

            def conv(lin, name, f0, chunks):
                def sums(product):
                    for i in range(2 * chunks):
                        fs = slice(i // 2 * P, i // 2 * P + P)
                        cols, w = halves(i)
                        b = unit(UNIT[name] + i)
                        for c in range(C):
                            if i == 0:
                                pe.wait_ge(act_done, ACTS[lin] + c + 1)
                                pe.wait_ge(freed, UNIT[lin] + c + 1)
                            mm = product(b[:, 0:w], (h_hi[:, c, fs], h_lo[:, c, fs]),
                                         (adj_hi[0][:, c, cols], adj_lo[0][:, c, cols]), c == 0, c == C - 1)
                        mm.then_inc(filled, 1)

                with pe.If(any_large > 0):
                    sums(three)
                with pe.Else():
                    sums(by_exact)

            def after_conv(name, chunks):
                return lambda c: (ACTS[name] + 2 * (2 * chunks - (c < 2)), UNIT[name] + 2 * chunks - (c < 2))

            linear("lin_a", 1, W1C, after_turn("h3T"))
            conv("lin_a", "conv_a", 0, 2)
            linear("lin_b", 1, W2C, after_conv("conv_a", 2), at=K * W1C, ks=(0, 1))
            conv("lin_b", "conv_b", 2, 1)
            linear("lin_c", 1, W3C, after_conv("conv_b", 1), at=K * W1C + 2 * W2C, ks=(2,))
            conv("lin_c", "conv_c", 3, 1)
            pe.wait_ge(w_split, 2 * 3 * (LAYERS + 1))
            linear("last", 2, F, after_conv("conv_c", 1))

        @block.vector
        def _(dve):
            def bank(u):
                return ps[:, u % 8]

            def row_stats(c):
                dve.bn_stats(stats[:, c], x_res[:, c]).then_inc(ln_stats, 1)

            def norm(k):
                dve.wait_ge(ln_stats, 2 * C * k + C)
                for c in range(C):
                    dve.bn_aggr(mv[:, c], stats[:, c]).then_inc(ln_stats, 1)
                dve.wait_ge(ln_act, (1 + C) * k + 1)
                dve.reciprocal(rstd[:], std[:]).then_inc(ln_coef, 1)
                dve.wait_ge(ln_coef, 2 * k + 1)
                dve.scalar_tensor_tensor(out=shift[:], in0=mv[:, :, 0], scalar=-1.0, in1=rstd[:],
                                         op0=ALU.mult, op1=ALU.mult).then_inc(ln_coef, 1)

            chain = [0]

            def link(ins):
                chain[0] += 1
                ins.then_inc(sort_step, 1)
                dve.wait_ge(sort_step, chain[0])

            dve.wait_ge(edges_in, 32)
            dve.wait_ge(consts_ready, 12)
            link(dve.tensor_copy(src_f[:], src_i[:]))
            dve.memset(reach[:, 0], 1.0).then_inc(rows_part, 1)
            dve.memset(reach[:, C], 0.0).then_inc(rows_part, 1)
            for b in range(1, C):
                dve.tensor_scalar(reach[:, b], src_f[:], float(b * NC), None, ALU.is_ge).then_inc(rows_part, 1)
            dve.wait_ge(rows_part, C + 1)
            link(dve.tensor_tensor(member[:], reach[:, 0:C], reach[:, 1:C + 1], op=ALU.subtract))
            for b in range(C):
                dve.tensor_tensor_scan(rank[:, b], member[:, b], zeros[:], 0.0, ALU.add, ALU.add).then_inc(rows_part, 1)
            dve.wait_ge(rows_part, 2 * C + 1)
            dve.tensor_copy(counts32[:], rank[:, :, ET - 1]).then_inc(counts_ready, 1)
            dve.wait_ge(rank_mm, 2)
            link(dve.tensor_scalar(total_i[:], ps[0:EP, 1, 0:C], float(PAIR - 1), None, ALU.add))
            shift_by = PAIR.bit_length() - 1
            link(dve.tensor_scalar(chunks_i[:], total_i[:], shift_by, None, ALU.logical_shift_right))
            link(dve.tensor_copy(chunks_f[:], chunks_i[:]))
            link(dve.tensor_tensor_scan(upto[:], chunks_f[:], zeros[:, 0:C], 0.0, ALU.add, ALU.add))
            link(dve.tensor_tensor(first[:], upto[:], chunks_f[:], op=ALU.subtract))
            link(dve.scalar_tensor_tensor(out=offset[:], in0=first[:], scalar=float(PAIR), in1=ps[0:EP, 0, 0:C],
                                          op0=ALU.mult, op1=ALU.add))
            dve.tensor_reduce(bucket[:], reach[:, 1:C].rearrange("p b t -> p t b"), axis=AX,
                              op=ALU.add).then_inc(ranks_read, 1)
            for b in range(C):
                dve.scalar_tensor_tensor(out=rank[:, b], in0=rank[:, b], scalar=offset[:, b:b + 1],
                                         in1=member[:, b], op0=ALU.add, op1=ALU.mult).then_inc(rows_part, 1)
            dve.wait_ge(rows_part, 3 * C + 1)
            link(dve.tensor_reduce(pos_f[:], rank[:].rearrange("p b t -> p t b"), axis=AX, op=ALU.add))
            link(dve.tensor_scalar(pos_i[:], pos_f[:], -1.0, None, ALU.add))
            link(dve.tensor_scalar(pos_lo[:], pos_i[:], P - 1, None, ALU.bitwise_and))
            link(dve.tensor_scalar(pos_hi[:], pos_i[:], P.bit_length() - 1, None, ALU.logical_shift_right))
            dve.scalar_tensor_tensor(out=row_i[:], in0=pos_lo[:], scalar=float(TILES), in1=pos_hi[:],
                                     op0=ALU.mult, op1=ALU.add).then_inc(rows_part, 1)
            dve.wait_ge(ranks_read, 1)
            link(dve.scalar_tensor_tensor(out=pos_f[:], in0=bucket[:], scalar=-float(NC), in1=src_f[:],
                                          op0=ALU.mult, op1=ALU.add))
            dve.tensor_scalar(fields[:, :, 1], pos_f[:], 1.0, None, ALU.add).then_inc(rows_part, 1)
            dve.tensor_copy(fields[:, :, 2], dst_i[:]).then_inc(rows_part, 1)
            dve.tensor_copy(fields[:, :, 3], dst_i[:]).then_inc(rows_part, 1)
            def limbs():
                dve.tensor_scalar(limb_i[:, 0], fields[:, 0:PERM, 0], LIMB_SHIFT, None,
                                  ALU.logical_shift_right).then_inc(rows_part, 1)
                dve.tensor_scalar(limb_i[:, 1], fields[:, 0:PERM, 0], LIMB_MASK, None, ALU.bitwise_and).then_inc(rows_part, 1)
                dve.tensor_copy(slot_lo[:], pos_lo[:, 0:PERM]).then_inc(rows_part, 1)
                dve.tensor_copy(slot_hi[:], pos_hi[:, 0:PERM]).then_inc(rows_part, 1)
                dve.tensor_copy(limb[:, 2], dst_i[:, 0:PERM]).then_inc(rows_part, 1)
                dve.wait_ge(rows_part, 3 * C + 10)
                dve.tensor_copy(limb[:, 0], limb_i[:, 0]).then_inc(rows_part, 1)
                dve.scalar_tensor_tensor(out=limb[:, 1], in0=limb_i[:, 1], scalar=float(P), in1=fields[:, 0:PERM, 1],
                                         op0=ALU.mult, op1=ALU.add).then_inc(rows_part, 1)
                dve.wait_ge(rows_part, 3 * C + 12)
                dve.sem_inc(limbs_ready, 1)

            def weights_low(start, end):
                for i in range(start, end):
                    high, low, raw = WEIGHTS[i]
                    dve.wait_ge(weights_hi, i + 1)
                    dve.tensor_tensor(low[:], raw[:], high[:], op=ALU.subtract).then_inc(weights_lo, 1)

            def fold(m):
                wait_rounds(dve, fold_mm, m, K)
                for k in range(K):
                    dve.wait_ge(split_hi, m * K + k + 1)
                    dve.tensor_tensor(fold_lo[:, :, k], stage[:, :, k], fold_hi[:, :, k],
                                      op=ALU.subtract).then_inc(split_lo, 1)
                if isinstance(m, int):
                    limbs()
                    weights_low(0, 2)
                    dve.wait_ge(x_in, 16)
                    for c in range(C):
                        row_stats(c)
                    norm(0)
                for i in range(PERM_FOLD):
                    col = bass.ds(m * PERM_FOLD + i, 1)
                    if not isinstance(m, int) or m > 0 or i >= PERM_RING:
                        dve.wait_ge(perm_mm, m * PERM_FOLD + (i - PERM_RING + 1))
                    dve.tensor_scalar(hot_lo[i % PERM_RING][:], iota_d[0:EP, 0:P], slot_lo[:, col], None,
                                      ALU.is_equal).then_inc(hots_made, 1)
                    dve.tensor_scalar(hot_hi[i % PERM_RING][:], iota_d[0:EP, 0:TILES], slot_hi[:, col], None,
                                      ALU.is_equal).then_inc(hots_made, 1)
                    dve.tensor_scalar(marked[i % PERM_RING][:, 0], iota_d[0:EP, 0:TILES], slot_hi[:, col],
                                      limb[:, 0, col], ALU.is_equal, ALU.mult).then_inc(hots_made, 1)

            each(dve, FOLDS, fold)
            link(dve.tensor_scalar(bucket_f[0][:], step_row[:], first[0:1, 1:2], None, ALU.is_ge))
            for b in range(2, C):
                o = bucket_f[(b + 1) % 2] if b < C - 1 else bucket_row
                link(dve.scalar_tensor_tensor(out=o[:], in0=step_row[:], scalar=first[0:1, b:b + 1],
                                              in1=bucket_f[b % 2][:], op0=ALU.is_ge, op1=ALU.add))

            dve.wait_ge(perm_mm, PERM)
            perm3 = ps[:, 5, 0:3 * TILES].rearrange("p (b t) -> p b t", b=3)
            dve.tensor_copy(perm_i[:, 0], perm3[:, 1]).then_inc(perm_out, 1)
            dve.wait_ge(perm_out, 1)
            dve.tensor_scalar(perm_i[:, 1], perm_i[:, 0], LIMB_BITS, None, ALU.logical_shift_right).then_inc(perm_out, 1)
            dve.tensor_scalar(perm_i[:, 2], perm_i[:, 0], P - 1, None, ALU.bitwise_and).then_inc(perm_out, 1)
            dve.wait_ge(perm_out, 3)
            dve.scalar_tensor_tensor(out=perm_e[:], in0=perm3[:, 0], scalar=float(LIMB_MASK + 1), in1=perm_i[:, 1],
                                     op0=ALU.mult, op1=ALU.add).then_inc(perm_out, 1)
            dve.wait_ge(perm_out, 4)
            dve.wait_ge(table_in, 16)
            for field, part in enumerate((perm_e[:], perm_i[:, 2], perm3[:, 2])):
                dve.tensor_tensor(table[:, :, field], table[:, :, field], part, op=ALU.add).then_inc(table_ready, 1)
            dve.wait_ge(table_ready, 3)
            dve.tensor_copy(srccol[:], table[:, :, 1]).then_inc(cols_ready, 1)
            dve.tensor_copy(dstcol[:], table[:, :, 2]).then_inc(cols_ready, 1)
            dve.wait_ge(cols_ready, 2)
            weights_low(2, 4)
            dve.wait_ge(split_lo, K * FOLDS)
            dve.wait_ge(consts_ready, 14)

            def rows_lo(t):
                s = t.slot
                dve.wait_ge(rT_hi_ready, t.count(1, 1))
                dve.tensor_tensor(rT_lo[s][:], ps[:, 0, 0:PAIR], rT_hi[s][:], op=ALU.subtract).then_inc(rT_lo_ready, 1)

            def edge_feature(t, j):
                dve.wait_ge(feat_mm, t.count(2, j + 1))
                t.wait(dve, msg_ready, 2, j - 1)
                dve.tensor_tensor(feat[j][:], ps[:, 3 + j], row_a[:], op=ALU.add).then_inc(feat_ready, 1)

            def message(t, j):
                s = t.slot
                dve.wait_ge(feat_ready, t.count(2, j + 1))
                dve.wait_ge(xg_in[s], t.rounds(32))
                t.wait(dve, m_lo_ready, 2, j - 1)
                dve.tensor_tensor(msg[j][:], feat[j][:], xg[s][:, j], op=ALU.mult).then_inc(msg_ready, 1)

            def message_lo(t, j):
                s = t.slot
                dve.wait_ge(m_hi_ready, t.count(2, j + 1))
                dve.tensor_tensor(m_lo[s][:, j], msg[j][:], m_hi[s][:, j], op=ALU.subtract).then_inc(m_lo_ready, 1)

            def one_hots(t):
                s = t.slot
                t.wait(dve, scat_mm, 2, -2)
                for j in range(2):
                    col = t.count(2, j)
                    dve.tensor_scalar(oh_src[s][:, j], iota_s[:], srccol[:, bass.ds(col, 1)], None,
                                      ALU.is_equal).then_inc(hots_ready, 1)
                    dve.tensor_scalar(oh_srcb[s][:, j], iota_s[:], srccol[:, bass.ds(col, 1)], None,
                                      ALU.is_equal).then_inc(hots_ready, 1)
                    dve.tensor_scalar(oh_dst[s][:, j], iota_d[:], dstcol[:, bass.ds(col, 1)], None,
                                      ALU.is_equal).then_inc(hots_ready, 1)

            def flush(t):
                b = dve.value_load(bucket_row[0:1, bass.ds(t.count(1), 1)], min_val=0, max_val=C - 1)
                agg = acc_agg[:, bass.ds(b * F, F)]
                adj = acc_adj[:, bass.ds(b * NP, NP)]
                dve.wait_ge(scat_mm, t.count(2, 1))
                t.wait(dve, flushed, 2, -1)
                dve.tensor_tensor(agg, ps[0:NC, 5], agg, op=ALU.add).then_inc(flushed, 1)
                dve.wait_ge(scat_mm, t.count(2, 2))
                t.wait(dve, flushed, 2)
                dve.tensor_tensor(adj, ps[0:NC, 6:8].rearrange("p b n -> p (b n)")[:, 0:NP], adj,
                                  op=ALU.add).then_inc(flushed, 1)

            rows_lo(Step(None, 0))
            rows_lo(Step(None, 1))
            weights_low(4, 5)

            def edge_step(t):
                one_hots(t)
                edge_feature(t, 0)
                message(t, 0)
                if t.reg is not None or t.c + 2 < STEPS:
                    rows_lo(t.at(2))
                message_lo(t, 0)
                edge_feature(t, 1)
                message(t, 1)
                if t.reg is not None or t.c > 0:
                    flush(t.at(-1))
                message_lo(t, 1)

            steps(dve, STEPS, edge_step)
            flush(Step(None, STEPS - 1))

            def halves(i):
                w = HALF[i % 2]
                return slice((i % 2) * HALF[0], (i % 2) * HALF[0] + w), w

            def turned_lo(name):
                for c in range(C):
                    n = slice(c * NC, c * NC + NC)
                    dve.wait_ge(act_done, ACTS[name] + c + 1)
                    dve.tensor_tensor(ht_lo[:, :, n],
                                      bank(UNIT[name] + c)[:, 0:K * NC].rearrange("p (k n) -> p k n", k=K),
                                      ht_hi[:, :, n], op=ALU.subtract).then_inc(freed, 1)

            turned_lo("aggT")
            for i in range(2 * K):
                cols, w = halves(i)
                dve.wait_ge(act_done, ACTS["mlp1"] + 2 * i + 2)
                dve.tensor_tensor(s1_lo[:, i // 2, cols], z32[:, i % 2, 0:w], s1_hi[:, i // 2, cols],
                                  op=ALU.subtract).then_inc(freed, 1)
            for i in range(2 * C):
                cols = slice(0, 4 * NC) if i % 2 == 0 else slice(4 * NC, N)
                w = 4 * NC if i % 2 == 0 else NC
                dve.wait_ge(act_done, ACTS["adjT"] + i + 1)
                dve.tensor_tensor(adj_lo[1][:, i // 2, cols], bank(UNIT["adjT"] + i)[0:NC, 0:w],
                                  adj_hi[1][:, i // 2, cols], op=ALU.subtract).then_inc(freed, 1)
            dve.tensor_reduce(part_col[:, 0], acc3, axis=AX, op=ALU.add).then_inc(deg_step, 1)
            for c in range(C):
                dve.wait_ge(filled, UNIT["mlp2"] + c + 1)
                dve.wait_ge(res_ready, 2 * C)
                dve.tensor_tensor(x_res[:, c], bank(UNIT["mlp2"] + c)[0:NC], x_res[:, c], op=ALU.add).then_inc(freed, 1)
                dve.wait_ge(freed, UNIT["mlp2"] + c + 1)
                row_stats(c)
            norm(1)
            turned_lo("h1T")
            dve.tensor_reduce(peaks[:], acc3, axis=AX, op=ALU.max).then_inc(peak_step, 1)
            dve.wait_ge(peak_step, 1)
            dve.tensor_reduce(peak[:], peaks[:], axis=AX, op=ALU.max).then_inc(peak_step, 1)
            dve.wait_ge(peak_step, 2)
            dve.tensor_scalar(large[:], peak[:].to_broadcast([NC, 2]), 4095.0, None, ALU.is_gt).then_inc(peak_step, 1)

            def out_and_turned(count, bank_of, acts):
                for i, (what, c, at) in enumerate(WOVEN):
                    if what == "out":
                        dve.wait_ge(act_done, acts(i + 1))
                        dve.scalar_tensor_tensor(out=h_lo[:, c], in0=bank_of(at)[0:NC], scalar=0.0, in1=h_hi[:, c],
                                                 op0=ALU.max, op1=ALU.subtract).then_inc(freed, 1)
                    else:
                        dve.wait_ge(filled, count(at + 2))
                        dve.wait_ge(act_done, acts(i + 1))
                        dve.tensor_copy(ht_lo[:, :, c * NC:c * NC + NC],
                                        bank_of(at + 1)[:, 0:K * NC].rearrange("p (k n) -> p k n", k=K)).then_inc(freed, 2)

            out_and_turned(lambda n: UNIT["init"] + n, lambda n: bank(UNIT["init"] + n), lambda n: ACTS["init"] + n)

            dve.wait_ge(filled, UNIT["large"] + 1)
            dve.tensor_copy(large_any[:], bank(UNIT["large"])[0:1, 0:1]).then_inc(freed, 1)

            for d in range(2):
                for i in range(2):
                    cols, w = halves(i)
                    dve.wait_ge(filled, UNIT["degrow"] + 2 * d + i + 1)
                    dve.tensor_scalar(z32[:, i, 0:w], bank(UNIT["degrow"] + 2 * d + i)[:, 0:w], 1.0, None,
                                      ALU.max).then_inc(freed, 1)
                for i in range(2):
                    cols, w = halves(i)
                    dve.wait_ge(freed, UNIT["degrow"] + 2 * d + i + 1)
                    dve.reciprocal(rdeg[d][:, cols], z32[:, i, 0:w]).then_inc(rdeg_ready, 1)
                dve.wait_ge(rdeg_ready, 2 * d + 2)


            def layer(l, last):
                def count(n):
                    return l * LAYER_UNITS + (UNIT["layer0"] + n)

                def acts(n):
                    return l * LAYER_ACTS + (ACTS["layer0"] + n)

                def scale(i):
                    d = i // 8
                    cols, w = halves(i)
                    dve.wait_ge(filled, count(i + 1))
                    if i < 2:
                        dve.wait_ge(freed, count(0))
                    else:
                        dve.wait_ge(z_lo_ready, l * 16 + i - 1)
                    dve.tensor_tensor(z32[:, i % 2, 0:w], ps[:, i % 8, 0:w], rdeg[d][:, cols], op=ALU.mult).then_inc(freed, 1)

                def low(i):
                    cols, w = halves(i)
                    d, f = i // 8, i % 8 // 2
                    dve.wait_ge(act_done, acts(i + 1))
                    dve.tensor_tensor(z_lo[d][:, f, cols], z32[:, i % 2, 0:w], z_hi[d][:, f, cols],
                                      op=ALU.subtract).then_inc(z_lo_ready, 1)

                scale(0)
                for i in range(1, 16):
                    scale(i)
                    low(i - 1)
                low(15)
                dve.wait_ge(w_split, l * 6 + 5)
                dve.tensor_tensor(w_lo[2][:].rearrange("p k f -> p (k f)"), wstage[:],
                                  w_hi[2][:].rearrange("p k f -> p (k f)"), op=ALU.subtract).then_inc(w_split, 1)
                if last:
                    dve.wait_ge(pads_ready, 4)
                    dve.tensor_reduce(part_col[:, 1], adj_hi[1][:], axis=AX, op=ALU.add).then_inc(deg_step, 1)
                    dve.tensor_reduce(part_col[:, 2], adj_lo[1][:], axis=AX, op=ALU.add).then_inc(deg_step, 1)
                    dve.wait_ge(deg_step, 3)
                    dve.tensor_scalar(deg_col[:, 0], part_col[:, 0], 1.0, None, ALU.add).then_inc(deg_step, 1)
                    dve.scalar_tensor_tensor(out=deg_col[:, 1], in0=part_col[:, 1], scalar=1.0, in1=part_col[:, 2],
                                             op0=ALU.add, op1=ALU.add).then_inc(deg_step, 1)
                    for c in range(C):
                        dve.wait_ge(filled, count(17 + c))
                        dve.scalar_tensor_tensor(out=x_res[:, c], in0=ps[0:NC, (16 + c) % 8], scalar=0.0,
                                                 in1=x_res[:, c], op0=ALU.max, op1=ALU.add).then_inc(freed, 1)
                        dve.wait_ge(freed, count(17 + c))
                        row_stats(c)
                    return
                out_and_turned(lambda n: count(16 + n), lambda n: ps[:, (16 + n) % 8], lambda n: acts(16 + n))

            with dve.Fori(0, LAYERS - 1) as l:
                layer(l, False)
            layer(LAYERS - 1, True)

            norm(2)
            dve.wait_ge(deg_root, 1)
            dve.reciprocal(dinv_col[:], root_col[:]).then_inc(deg_step, 1)
            turned_lo("h2T")
            dve.wait_ge(bias2_in, 16)
            for c in range(C):
                dve.wait_ge(filled, UNIT["lin2"] + c + 1)
                dve.tensor_tensor(g32[:, c], bank(UNIT["lin2"] + c)[0:NC], row_a[0:NC], op=ALU.add).then_inc(freed, 1)
            for c in range(C):
                dve.wait_ge(freed, UNIT["lin2"] + c + 1)
                dve.wait_ge(act_done, ACTS["lin2"] + c + 1)
                dve.scalar_tensor_tensor(out=h_lo[:, c], in0=g32[:, c], scalar=dinv_col[:, 0, c:c + 1],
                                         in1=h_hi[:, c], op0=ALU.mult, op1=ALU.subtract).then_inc(split_g, 1)
            for c in range(C):
                dve.wait_ge(filled, UNIT["conv2"] + c + 1)
                dve.wait_ge(split_g, C)
                dve.tensor_scalar(g32[:, c], bank(UNIT["conv2"] + c)[0:NC], dinv_col[:, 0, c:c + 1], 0.0,
                                  ALU.mult, ALU.max).then_inc(freed, 1)
                dve.wait_ge(freed, UNIT["conv2"] + c + 1)
                dve.tensor_tensor(x_res[:, c], x_res[:, c], g32[:, c], op=ALU.add).then_inc(scaled_x, 1)
                dve.wait_ge(scaled_x, c + 1)
                row_stats(c)
            for i in range(2):
                cols, w = halves(i)
                dve.wait_ge(filled, UNIT["sumrow"] + i + 1)
                dve.tensor_scalar(deg_row[:, cols], bank(UNIT["sumrow"] + i)[:, 0:w], 1.0, None, ALU.max).then_inc(freed, 1)
            norm(3)
            dve.wait_ge(act_done, ACTS["sumrow"] + 2)
            dve.reciprocal(dinv_row[:], root_row[:]).then_inc(rdeg_ready, 1)
            dve.wait_ge(rdeg_ready, 5)
            dve.wait_ge(bias4_in, 16)
            dve.wait_ge(ln_act, 4 * (1 + C))
            for c in range(C):
                dve.tensor_tensor(x_res[:, c], x_res[:, c], row_b[0:NC], op=ALU.add).then_inc(scaled_x, 1)
            turned_lo("h3T")

            def conv(lin, name, f0, chunks):
                for c in range(C):
                    w = chunks * P
                    dve.wait_ge(act_done, ACTS[lin] + c + 1)
                    dve.scalar_tensor_tensor(out=h_lo[:, c, 0:w], in0=bank(UNIT[lin] + c)[0:NC, 0:w],
                                             scalar=dinv_col[:, 1, c:c + 1], in1=h_hi[:, c, 0:w],
                                             op0=ALU.mult, op1=ALU.subtract).then_inc(freed, 1)
                for i in range(2 * chunks):
                    cols, w = halves(i)
                    f = f0 + i // 2
                    dve.wait_ge(filled, UNIT[name] + i + 1)
                    if i >= 2:
                        dve.wait_ge(act_done, ACTS[name] + 2 * i - 3)
                    dve.tensor_tensor(z32[:, i % 2, 0:w], bank(UNIT[name] + i)[:, 0:w], dinv_row[:, cols],
                                      op=ALU.mult).then_inc(scaled, 1)
                    dve.wait_ge(act_done, ACTS[name] + 2 * i + 2)
                    dve.tensor_tensor(ht_lo[:, f, cols], relu32[:, i % 2, 0:w], ht_hi[:, f, cols],
                                      op=ALU.subtract).then_inc(freed, 1)

            conv("lin_a", "conv_a", 0, 2)
            conv("lin_b", "conv_b", 2, 1)
            conv("lin_c", "conv_c", 3, 1)
            dve.wait_ge(scaled_x, 2 * C)
            for c in range(C):
                dve.wait_ge(filled, UNIT["last"] + c + 1)
                dve.tensor_tensor(x_res[:, c], bank(UNIT["last"] + c)[0:NC], x_res[:, c], op=ALU.add).then_inc(freed, 1)


def kernel(**inputs):
    import numpy as np
    import concourse.bacc as bacc
    from concourse.bass_utils import run_bass_kernel_spmd

    def packed(w):
        return w.reshape(-1, P, w.shape[1]).transpose(1, 0, 2).reshape(P, -1)

    g = {name: np.asarray(v) for name, v in inputs.items()}
    w_self = g["L1_gnn_W_self"]
    fold_a, fold_b, selfw = [], [], []
    for l in range(LAYERS):
        t = w_self[l].T
        selfw.append(packed(t[0:F]))
        fold_a += [packed(g["L1_gnn_W_fwd"][l]), packed(g["L1_gnn_W_bwd"][l])]
        fold_b += [packed(t[F:2 * F]), packed(t[2 * F:3 * F])]
    conv_w = np.concatenate([packed(g["L3_gnn_W1"]), packed(g["L3_gnn_W2"]), packed(g["L3_gnn_W3"])], axis=1)
    conv_w = np.concatenate([conv_w, np.zeros((P, K * F - conv_w.shape[1]), conv_w.dtype)], axis=1)
    conv_bias = np.concatenate([g["L3_gnn_b1"], g["L3_gnn_b2"], g["L3_gnn_b3"]]).reshape(4, P).T
    data = {
        "x": g["x"], "src": g["src"].reshape(EP, ET), "dst": g["dst"].reshape(EP, ET),
        "edge": g["edge_attr_128"],
        "we1": g["L0_gnn_We1"], "be1": g["L0_gnn_be1"].reshape(K, P).T,
        "we2": packed(g["L0_gnn_We2"]), "be2": g["L0_gnn_be2"].reshape(1, F),
        "nodew": np.stack([packed(g["L0_gnn_Wn1"]), packed(g["L0_gnn_Wn2"]), packed(g["L1_gnn_W_init"].T)]),
        "bn1": g["L0_gnn_bn1"].reshape(K, P).T, "bn2": g["L0_gnn_bn2"].reshape(1, F),
        "fold_a": np.stack(fold_a), "fold_b": np.stack(fold_b), "selfw": np.stack(selfw),
        "lin2": packed(g["L2_gnn_W"].T), "b2": g["L2_gnn_b"].reshape(1, F),
        "conv_w": conv_w, "conv_bias": conv_bias,
        "lastw": packed(g["L3_gnn_W4"].T), "b4": g["L3_gnn_b4"].reshape(1, F),
    }
    nc = bacc.Bacc("TRN2", target_bir_lowering=False, num_devices=1)
    arrays, args = {}, {}
    for name, v in data.items():
        v = np.ascontiguousarray(v)
        arrays[f"in_{name}"] = v
        args[name] = nc.dram_tensor(f"in_{name}", v.shape, mybir.dt.from_np(v.dtype), kind="ExternalInput").ap()
    out = nc.dram_tensor("out_0", (N, F), F32, kind="ExternalOutput").ap()
    build(nc, args, out)
    r = run_bass_kernel_spmd(nc, [arrays], core_ids=[0])
    return r.results[0]["out_0"]
```
